# Optimizing a Trainium2 kernel written in Bass

```python
import numpy as np
import jax
import jax.numpy as jnp

def _softmax(x, axis=-1):
    return jax.nn.softmax(x, axis=axis)

def _gelu(x):
    return jax.nn.gelu(x, approximate=True)

def _silu(x):
    return jax.nn.silu(x)

def _sigmoid(x):
    return jax.nn.sigmoid(x)

def _layernorm(x, axis=-1, eps=1e-05):
    m = jnp.mean(x, axis=axis, keepdims=True)
    v = jnp.var(x, axis=axis, keepdims=True)
    return (x - m) / jnp.sqrt(v + eps)

def _scatter_add(tgt, idx, src, axis=0):
    return tgt.at[idx].add(src)

def _segment_sum(src, seg, n):
    return jax.ops.segment_sum(src, seg, n)
kernel_name = 'mk_prb_d1_jaxref_r8_7717f1'

def setup_inputs(seed: int=0):
    np.random.seed(seed)
    _w = jnp.asarray

    def _L0_attn_setup():
        import jax, jax.numpy as jnp
        import numpy as np
        EPS_NORM = 1e-05
        EPS_L2 = 1e-06
        CHUNK = 128

        def _short_conv(x, w):
            K = w.shape[1]
            T = x.shape[1]
            xp = jnp.pad(x, ((0, 0), (K - 1, 0), (0, 0)))
            y = sum((xp[:, i:i + T, :] * w[:, i] for i in range(K)))
            return jax.nn.silu(y)

        def _l2norm(x):
            return x * jax.lax.rsqrt(jnp.sum(x * x, axis=-1, keepdims=True) + EPS_L2)

        def _kda_scan(q, k, v, gk, beta):
            B, T, H, Dk = q.shape
            Dv = v.shape[-1]
            NC = T // CHUNK

            def c4(x):
                return jnp.transpose(x.reshape(B, NC, CHUNK, H, x.shape[-1]), (1, 2, 0, 3, 4))
            qc, kc, vc, gc = (c4(q), c4(k), c4(v), c4(gk))
            bc = jnp.transpose(beta.reshape(B, NC, CHUNK, H), (1, 2, 0, 3))

            def step(S, inp):
                q_t, k_t, v_t, g_t, b_t = inp
                S = S * jnp.exp(g_t)[..., None]
                err = v_t - jnp.einsum('bhk,bhkv->bhv', k_t, S)
                S = S + b_t[..., None, None] * (k_t[..., None] * err[..., None, :])
                o_t = jnp.einsum('bhk,bhkv->bhv', q_t, S)
                return (S, o_t)

            @jax.checkpoint
            def chunk_fn(S, xs):
                return jax.lax.scan(step, S, xs)
            S0 = jnp.zeros((B, H, Dk, Dv), q.dtype)
            _, o = jax.lax.scan(chunk_fn, S0, (qc, kc, vc, gc, bc))
            return jnp.transpose(o.reshape(T, B, H, Dv), (1, 0, 2, 3))

        def _forward(hidden_states, q_w, k_w, v_w, q_conv_w, k_conv_w, v_conv_w, f_w1, f_w2, b_w, A_log, dt_bias, g_w1, g_w2, g_b2, o_norm_w, o_w):
            B, T, D = hidden_states.shape
            H = A_log.shape[0]
            Dv = o_norm_w.shape[0]
            Dk = q_w.shape[1] // H
            q = _short_conv(hidden_states @ q_w, q_conv_w).reshape(B, T, H, Dk)
            k = _short_conv(hidden_states @ k_w, k_conv_w).reshape(B, T, H, Dk)
            v = _short_conv(hidden_states @ v_w, v_conv_w).reshape(B, T, H, Dv)
            g = (hidden_states @ f_w1 @ f_w2).reshape(B, T, H, Dk)
            gk = -jnp.exp(A_log)[:, None] * jax.nn.softplus(g + dt_bias.reshape(H, Dk))
            beta = jax.nn.sigmoid(hidden_states @ b_w)
            q = _l2norm(q) * Dk ** (-0.5)
            k = _l2norm(k)
            o = _kda_scan(q, k, v, gk, beta)
            gate = (hidden_states @ g_w1 @ g_w2 + g_b2).reshape(B, T, H, Dv)
            o = o * jax.lax.rsqrt(jnp.mean(o * o, axis=-1, keepdims=True) + EPS_NORM) * o_norm_w
            o = o * jax.nn.sigmoid(gate)
            return o.reshape(B, T, H * Dv) @ o_w
        key = jax.random.key(seed)
        B, T, D = (2, 512, 256)
        H, Dk, Dv = (16, 128, 128)
        KD, VD = (H * Dk, H * Dv)
        Kc = 4
        ks = jax.random.split(key, 16)
        s = 0.02
        n = lambda kk, sh: jax.random.normal(kk, sh, jnp.float32) * s
        return dict(hidden_states=jax.random.normal(ks[0], (B, T, D), jnp.float32), q_w=n(ks[1], (D, KD)), k_w=n(ks[2], (D, KD)), v_w=n(ks[3], (D, VD)), q_conv_w=n(ks[4], (KD, Kc)), k_conv_w=n(ks[5], (KD, Kc)), v_conv_w=n(ks[6], (VD, Kc)), f_w1=n(ks[7], (D, Dv)), f_w2=n(ks[8], (Dv, KD)), b_w=n(ks[9], (D, H)), A_log=jnp.log(jax.random.uniform(ks[10], (H,), jnp.float32, 1.0, 16.0)), dt_bias=jnp.zeros((KD,), jnp.float32), g_w1=n(ks[11], (D, Dv)), g_w2=n(ks[12], (Dv, VD)), g_b2=jnp.zeros((VD,), jnp.float32), o_norm_w=jnp.ones((Dv,), jnp.float32), o_w=n(ks[13], (VD, D)))
    _L0_attn_in = _L0_attn_setup()

    def _L0_ffn_setup():
        import jax, jax.numpy as jnp
        import numpy as np
        HIDDEN = 256
        INTER = 1024
        SCALE = 64.0

        def fwht(x):
            orig_shape = x.shape
            n = orig_shape[-1]
            x = x.reshape(-1, n)
            h = 1
            while h < n:
                x = x.reshape(-1, n // (2 * h), 2, h)
                a, b = (x[:, :, 0, :], x[:, :, 1, :])
                x = jnp.stack([a + b, a - b], axis=2).reshape(-1, n)
                h *= 2
            return (x / jnp.sqrt(jnp.asarray(n, x.dtype))).reshape(orig_shape)
        key = jax.random.key(seed)
        ks = jax.random.split(key, 8)
        inp = jax.random.normal(ks[0], (4, 256, HIDDEN), dtype=jnp.float32)
        SU_ug = jnp.where(jax.random.bernoulli(ks[1], 0.5, (HIDDEN,)), 1.0, -1.0).astype(jnp.float32)
        SU_dp = jnp.where(jax.random.bernoulli(ks[2], 0.5, (INTER,)), 1.0, -1.0).astype(jnp.float32)
        Wscale_ug = jax.random.uniform(ks[3], (2 * INTER,), jnp.float32, 0.5, 1.5)
        Wscale_dp = jax.random.uniform(ks[4], (HIDDEN,), jnp.float32, 0.5, 1.5)
        W_up = jax.random.normal(ks[5], (INTER, HIDDEN), dtype=jnp.float32) * 0.02
        W_gate = jax.random.normal(ks[6], (INTER, HIDDEN), dtype=jnp.float32) * 0.02
        W_down = jax.random.normal(ks[7], (HIDDEN, INTER), dtype=jnp.float32) * 0.02
        return {'input': inp, 'SU_ug': SU_ug, 'SU_dp': SU_dp, 'Wscale_ug': Wscale_ug, 'Wscale_dp': Wscale_dp, 'W_up': W_up, 'W_gate': W_gate, 'W_down': W_down}
    _L0_ffn_in = _L0_ffn_setup()
    _d = {'L0_attn_hidden_states': _L0_attn_in['hidden_states'], 'L0_attn_q_w': _L0_attn_in['q_w'], 'L0_attn_k_w': _L0_attn_in['k_w'], 'L0_attn_v_w': _L0_attn_in['v_w'], 'L0_attn_q_conv_w': _L0_attn_in['q_conv_w'], 'L0_attn_k_conv_w': _L0_attn_in['k_conv_w'], 'L0_attn_v_conv_w': _L0_attn_in['v_conv_w'], 'L0_attn_f_w1': _L0_attn_in['f_w1'], 'L0_attn_f_w2': _L0_attn_in['f_w2'], 'L0_attn_b_w': _L0_attn_in['b_w'], 'L0_attn_A_log': _L0_attn_in['A_log'], 'L0_attn_dt_bias': _L0_attn_in['dt_bias'], 'L0_attn_g_w1': _L0_attn_in['g_w1'], 'L0_attn_g_w2': _L0_attn_in['g_w2'], 'L0_attn_g_b2': _L0_attn_in['g_b2'], 'L0_attn_o_norm_w': _L0_attn_in['o_norm_w'], 'L0_attn_o_w': _L0_attn_in['o_w'], 'L0_ffn_SU_ug': _L0_ffn_in['SU_ug'], 'L0_ffn_SU_dp': _L0_ffn_in['SU_dp'], 'L0_ffn_Wscale_ug': _L0_ffn_in['Wscale_ug'], 'L0_ffn_Wscale_dp': _L0_ffn_in['Wscale_dp'], 'L0_ffn_W_up': _L0_ffn_in['W_up'], 'L0_ffn_W_gate': _L0_ffn_in['W_gate'], 'L0_ffn_W_down': _L0_ffn_in['W_down']}
    _x0 = _d['L0_attn_hidden_states']
    _d['L0_attn_hidden_states'] = jax.random.normal(jax.random.fold_in(jax.random.key(seed), 1), (2, 512, 256), dtype=_x0.dtype)
    del _x0
    return _d

def reference(L0_attn_hidden_states, L0_attn_q_w, L0_attn_k_w, L0_attn_v_w, L0_attn_q_conv_w, L0_attn_k_conv_w, L0_attn_v_conv_w, L0_attn_f_w1, L0_attn_f_w2, L0_attn_b_w, L0_attn_A_log, L0_attn_dt_bias, L0_attn_g_w1, L0_attn_g_w2, L0_attn_g_b2, L0_attn_o_norm_w, L0_attn_o_w, L0_ffn_SU_ug, L0_ffn_SU_dp, L0_ffn_Wscale_ug, L0_ffn_Wscale_dp, L0_ffn_W_up, L0_ffn_W_gate, L0_ffn_W_down):

    def _L0_attn_ref(hidden_states, q_w, k_w, v_w, q_conv_w, k_conv_w, v_conv_w, f_w1, f_w2, b_w, A_log, dt_bias, g_w1, g_w2, g_b2, o_norm_w, o_w):
        import jax, jax.numpy as jnp
        import numpy as np
        EPS_NORM = 1e-05
        EPS_L2 = 1e-06
        CHUNK = 128

        def _short_conv(x, w):
            K = w.shape[1]
            T = x.shape[1]
            xp = jnp.pad(x, ((0, 0), (K - 1, 0), (0, 0)))
            y = sum((xp[:, i:i + T, :] * w[:, i] for i in range(K)))
            return jax.nn.silu(y)

        def _l2norm(x):
            return x * jax.lax.rsqrt(jnp.sum(x * x, axis=-1, keepdims=True) + EPS_L2)

        def _kda_scan(q, k, v, gk, beta):
            B, T, H, Dk = q.shape
            Dv = v.shape[-1]
            NC = T // CHUNK

            def c4(x):
                return jnp.transpose(x.reshape(B, NC, CHUNK, H, x.shape[-1]), (1, 2, 0, 3, 4))
            qc, kc, vc, gc = (c4(q), c4(k), c4(v), c4(gk))
            bc = jnp.transpose(beta.reshape(B, NC, CHUNK, H), (1, 2, 0, 3))

            def step(S, inp):
                q_t, k_t, v_t, g_t, b_t = inp
                S = S * jnp.exp(g_t)[..., None]
                err = v_t - jnp.einsum('bhk,bhkv->bhv', k_t, S)
                S = S + b_t[..., None, None] * (k_t[..., None] * err[..., None, :])
                o_t = jnp.einsum('bhk,bhkv->bhv', q_t, S)
                return (S, o_t)

            @jax.checkpoint
            def chunk_fn(S, xs):
                return jax.lax.scan(step, S, xs)
            S0 = jnp.zeros((B, H, Dk, Dv), q.dtype)
            _, o = jax.lax.scan(chunk_fn, S0, (qc, kc, vc, gc, bc))
            return jnp.transpose(o.reshape(T, B, H, Dv), (1, 0, 2, 3))

        def _forward(hidden_states, q_w, k_w, v_w, q_conv_w, k_conv_w, v_conv_w, f_w1, f_w2, b_w, A_log, dt_bias, g_w1, g_w2, g_b2, o_norm_w, o_w):
            B, T, D = hidden_states.shape
            H = A_log.shape[0]
            Dv = o_norm_w.shape[0]
            Dk = q_w.shape[1] // H
            q = _short_conv(hidden_states @ q_w, q_conv_w).reshape(B, T, H, Dk)
            k = _short_conv(hidden_states @ k_w, k_conv_w).reshape(B, T, H, Dk)
            v = _short_conv(hidden_states @ v_w, v_conv_w).reshape(B, T, H, Dv)
            g = (hidden_states @ f_w1 @ f_w2).reshape(B, T, H, Dk)
            gk = -jnp.exp(A_log)[:, None] * jax.nn.softplus(g + dt_bias.reshape(H, Dk))
            beta = jax.nn.sigmoid(hidden_states @ b_w)
            q = _l2norm(q) * Dk ** (-0.5)
            k = _l2norm(k)
            o = _kda_scan(q, k, v, gk, beta)
            gate = (hidden_states @ g_w1 @ g_w2 + g_b2).reshape(B, T, H, Dv)
            o = o * jax.lax.rsqrt(jnp.mean(o * o, axis=-1, keepdims=True) + EPS_NORM) * o_norm_w
            o = o * jax.nn.sigmoid(gate)
            return o.reshape(B, T, H * Dv) @ o_w
        return _forward(hidden_states, q_w, k_w, v_w, q_conv_w, k_conv_w, v_conv_w, f_w1, f_w2, b_w, A_log, dt_bias, g_w1, g_w2, g_b2, o_norm_w, o_w)

    def _L0_ffn_ref(input, SU_ug, SU_dp, Wscale_ug, Wscale_dp, W_up, W_gate, W_down):
        import jax, jax.numpy as jnp
        import numpy as np
        HIDDEN = 256
        INTER = 1024
        SCALE = 64.0

        def fwht(x):
            orig_shape = x.shape
            n = orig_shape[-1]
            x = x.reshape(-1, n)
            h = 1
            while h < n:
                x = x.reshape(-1, n // (2 * h), 2, h)
                a, b = (x[:, :, 0, :], x[:, :, 1, :])
                x = jnp.stack([a + b, a - b], axis=2).reshape(-1, n)
                h *= 2
            return (x / jnp.sqrt(jnp.asarray(n, x.dtype))).reshape(orig_shape)
        n = SU_ug.shape[0]
        x = input.reshape(-1, n)
        x = fwht(x * SU_ug) / SCALE
        x_up = x @ W_up.T * (Wscale_ug[:INTER] * SCALE)
        x_gate = x @ W_gate.T * (Wscale_ug[INTER:] * SCALE)
        x = jax.nn.silu(x_gate) * x_up
        x = fwht(x * SU_dp) / SCALE
        x = x @ W_down.T * (Wscale_dp * SCALE)
        return x.reshape(input.shape)
    x = L0_attn_hidden_states
    xn = _layernorm(x, axis=-1)
    x = x + _L0_attn_ref(xn, L0_attn_q_w, L0_attn_k_w, L0_attn_v_w, L0_attn_q_conv_w, L0_attn_k_conv_w, L0_attn_v_conv_w, L0_attn_f_w1, L0_attn_f_w2, L0_attn_b_w, L0_attn_A_log, L0_attn_dt_bias, L0_attn_g_w1, L0_attn_g_w2, L0_attn_g_b2, L0_attn_o_norm_w, L0_attn_o_w) + _L0_ffn_ref(xn, L0_ffn_SU_ug, L0_ffn_SU_dp, L0_ffn_Wscale_ug, L0_ffn_Wscale_dp, L0_ffn_W_up, L0_ffn_W_gate, L0_ffn_W_down)
    return x

_drawn_inputs = setup_inputs


def setup_inputs(seed=0):
    import zlib

    import numpy as np

    out = dict(_drawn_inputs(seed))
    spreads = {'L0_attn_dt_bias': (0.0, 2.0), 'L0_attn_g_b2': (0.0, 0.8), 'L0_attn_o_norm_w': (1.0, 0.6)}
    factors = {'L0_attn_q_w': 8.0,
     'L0_attn_k_w': 8.0,
     'L0_attn_v_w': 8.0,
     'L0_attn_q_conv_w': 8.0,
     'L0_attn_k_conv_w': 8.0,
     'L0_attn_v_conv_w': 8.0,
     'L0_attn_f_w1': 8.0,
     'L0_attn_f_w2': 8.0,
     'L0_attn_b_w': 8.0,
     'L0_attn_A_log': 8.0,
     'L0_attn_g_w1': 8.0,
     'L0_attn_g_w2': 8.0,
     'L0_attn_o_w': 8.0,
     'L0_ffn_Wscale_ug': 3.96,
     'L0_ffn_Wscale_dp': 5.509}
    for name, (base, spread) in spreads.items():
        noise = np.random.default_rng([zlib.crc32(name.encode()), seed]).standard_normal(out[name].shape)
        drawn = base * np.exp(spread * noise) if base else spread * noise
        out[name] = jnp.asarray(drawn.astype(out[name].dtype))
    for name, factor in factors.items():
        out[name] = (out[name] * factor).astype(out[name].dtype)
    return out
```

```python
from contextlib import ExitStack

import numpy as np
import concourse.bass as bass
from concourse import mybir

F32 = mybir.dt.float32
U32 = mybir.dt.uint32
ALU = mybir.AluOpType
ACT = mybir.ActivationFunctionType
AX_X = mybir.AxisListType.X

P = 128
BATCH, SEQ, D = 2, 512, 256
HEADS = 16
TOK = BATCH * SEQ
NCH = TOK // P
CPB = SEQ // P
KT = D // P
INTER = 1024
FT = INTER // P
TAPS = 4
LEVELS = 7
EPS_LN, EPS_L2, EPS_NORM = 1e-5, 1e-6, 1e-5

A_Q, A_K, A_F2, A_C = 0, KT * P, 2 * KT * P, 2 * KT * P + P
A_COLS = A_C + 16
B_V, B_G2, B_C = 0, KT * P, KT * P + P
B_COLS = B_C + 16
SC_PER_HEAD = LEVELS + 2
PJ_PREP, PJ_LEVEL, PJ_SCAN = 5, 3, 3


def wait(eng, sem, value):
    if isinstance(value, int) and value <= 0:
        return
    eng.wait_ge(sem, value)


def scaled_count(level):
    return 2 + 3 * level


def setup_block(nc, io, sb, ps, names):
    sem = {n: names.enter_context(nc.semaphore("setup_" + n)) for n in (
        "x_loaded", "const_loaded", "ffn_const_loaded", "small_w_loaded", "up_loaded", "gate_loaded", "down_loaded",
        "stats", "moments", "var", "rstd", "xn", "xn_T", "xn_T_copied", "signed_x", "x_mixed", "x_had", "x_had_copied",
        "w_scaled", "shared", "shared_copied", "beta_exp", "beta_step", "w_mixed", "w_had", "w_down_ready", "wdp_scaled",
        "gate_up", "silu", "y_ready", "down", "acc_ready", "hw_ready")}
    acc, xnT, lv, kq = sb["acc"], sb["xnT"], sb["lv"], sb["kq"]
    cst, ffc, small = sb["cst"], sb["oT"], sb["o_raw"]
    hadamard, ident = cst[:, 0:P], cst[:, P:2 * P]
    xn = [sb["vn"][n] for n in range(2)]
    y = lv[:, 0:FT * TOK].rearrange("p (f t) -> p f t", f=FT)
    w_up = lv[:, FT * TOK:FT * TOK + 2048].rearrange("p (k f) -> p k f", k=KT)
    w_gate = lv[:, FT * TOK + 2048:FT * TOK + 4096].rearrange("p (k f) -> p k f", k=KT)
    x_had = lv[:, FT * TOK + 4096:FT * TOK + 6144].rearrange("p (k t) -> p k t", k=KT)
    signed = [sb["g_sig"][0], sb["g_sig"][1]]
    mixed = [sb["k_hat"][0], sb["k_hat"][1]]
    wd = [kq[0], kq[1]]
    silu_t = [sb["q"], sb["a"]]
    su_ug, su_dp, wsc, wdp = ffc[:, 0:2], ffc[:, 2:10], ffc[:, 10:26], ffc[:, 32:288]
    wsc16, wdp32 = ffc[:, 288:304], ffc[:, 304:560]
    f_w1 = small[:, 0:256].rearrange("p (k n) -> p k n", k=KT)
    g_w1 = small[:, 256:512].rearrange("p (k n) -> p k n", k=KT)
    b_w = small[:, 512:544].rearrange("p (k n) -> p k n", k=KT)
    beta_tmp = small[:, 544:672]
    beta_tmp2 = small[:, 672:800]
    stats = [sb["v"][:, 16 * c:16 * c + 6] for c in range(NCH)]
    moments = [sb["v"][:, 128 + 4 * c:128 + 4 * c + 2] for c in range(NCH)]
    var_eps, rstd_all = sb["v"][:, 192:192 + NCH], sb["v"][:, 208:208 + NCH]
    rstd = [rstd_all[:, c:c + 1] for c in range(NCH)]

    def xn_tile(c):
        return xn[c // 4][:, (c % 4) * D:(c % 4 + 1) * D]

    with nc.Block() as block:
        @block.sync
        def _(sp):
            for c in range(NCH):
                sp.dma_start(acc[:, c, :], io["x"][c * P:(c + 1) * P, :]).then_inc(sem["x_loaded"], 16)
            sp.dma_start(cst[:, :], io["consts"]).then_inc(sem["const_loaded"], 16)
            sp.dma_start(sb["hw"][:, :], io["o_norm_w"]).then_inc(sem["const_loaded"], 16)
            sp.dma_start(small[:, 0:544], io["small_w"]).then_inc(sem["small_w_loaded"], 16)
            sp.dma_start(w_gate, io["w_gate"]).then_inc(sem["gate_loaded"], 16)
            sp.dma_start(w_up, io["w_up"]).then_inc(sem["up_loaded"], 16)

        @block.gpsimd
        def _(pool):
            pool.wait_ge(sem["var"], NCH)
            pool.tensor_tensor(rstd_all, var_eps, sb["powers"][:, 0:NCH], ALU.pow).then_inc(sem["rstd"], 1)

        @block.scalar
        def _(act):
            act.dma_start(ffc[:, 0:288], io["ffn_consts"]).then_inc(sem["ffn_const_loaded"], 16)
            act.dma_start(wd[0][:, :], io["w_down"]).then_inc(sem["down_loaded"], 16)
            for c in range(NCH):
                act.wait_ge(sem["xn_T"], c + 1)
                act.activation(xnT[:, :, c * P:(c + 1) * P],
                               ps[:, 512 * c:512 * c + 2 * P].rearrange("p (k t) -> p k t", k=KT),
                               ACT.Copy).then_inc(sem["xn_T_copied"], 1)
            for n, dst in enumerate((sb["f1T"], sb["g1T"])):
                act.wait_ge(sem["shared"], n + 1)
                act.activation(dst[:, :], ps[:, 1024 * n:1024 * n + 1024], ACT.Copy).then_inc(sem["shared_copied"], 1)
            act.wait_ge(sem["shared"], 3)
            act.activation(beta_tmp, ps[:, 2048:2176], ACT.Exp, scale=-1.0).then_inc(sem["beta_exp"], 1)
            for k in range(KT):
                act.wait_ge(sem["x_had"], k + 1)
                act.activation(x_had[:, k, :], ps[:, 1024 * k:1024 * (k + 1)], ACT.Copy).then_inc(sem["x_had_copied"], 1)
            act.wait_ge(sem["w_scaled"], 1)
            for f in range(FT):
                act.wait_ge(sem["gate_up"], f + 1)
                if f >= 2:
                    act.wait_ge(sem["y_ready"], f - 1)
                act.activation(silu_t[f % 2][:, :], ps[:, 2048 * (f % 2):2048 * (f % 2) + 1024], ACT.Silu,
                               scale=wsc16[:, FT + f:FT + f + 1]).then_inc(sem["silu"], 1)

        @block.vector
        def _(dve):
            for c in range(NCH):
                dve.wait_ge(sem["x_loaded"], 16 * NCH)
                dve.bn_stats(stats[c], acc[:, c, :]).then_inc(sem["stats"], 1)
            for c in range(NCH):
                dve.wait_ge(sem["stats"], c + 1)
                dve.bn_aggr(moments[c], stats[c]).then_inc(sem["moments"], 1)
            for c in range(NCH):
                dve.wait_ge(sem["moments"], c + 1)
                dve.tensor_scalar(var_eps[:, c:c + 1], moments[c][:, 1:2], EPS_LN, None, ALU.add)\
                   .then_inc(sem["var"], 1)
            for c in range(NCH):
                dve.wait_ge(sem["rstd"], 1)
                dve.tensor_scalar(xn_tile(c), acc[:, c, :], moments[c][:, 0:1], rstd[c], ALU.subtract,
                                  ALU.mult).then_inc(sem["xn"], 1)
            dve.wait_ge(sem["ffn_const_loaded"], 16)
            dve.tensor_scalar(wsc16, wsc, float(D) ** -0.5, None, ALU.mult).then_inc(sem["w_scaled"], 1)
            dve.tensor_scalar(wdp32, wdp, float(INTER) ** -0.5, None, ALU.mult).then_inc(sem["wdp_scaled"], 1)
            dve.wait_ge(sem["const_loaded"], 32)
            dve.tensor_scalar(sb["hw"][:, :], sb["hw"][:, :], 0.5, None, ALU.mult).then_inc(sem["hw_ready"], 1)
            dve.wait_ge(sem["xn_T_copied"], NCH)
            for k in range(KT):
                dve.tensor_scalar(signed[k][:, :], xnT[:, k, :], su_ug[:, k:k + 1], None, ALU.mult)\
                   .then_inc(sem["signed_x"], 1)
            dve.wait_ge(sem["signed_x"], 2)
            for k, op in enumerate((ALU.add, ALU.subtract)):
                dve.tensor_tensor(mixed[k][:, :], signed[0][:, :], signed[1][:, :], op).then_inc(sem["x_mixed"], 1)
            dve.wait_ge(sem["beta_exp"], 1)
            dve.tensor_scalar(beta_tmp2, beta_tmp, 1.0, None, ALU.add).then_inc(sem["beta_step"], 1)
            dve.wait_ge(sem["beta_step"], 1)
            dve.reciprocal(beta_tmp, beta_tmp2).then_inc(sem["beta_step"], 1)
            dve.wait_ge(sem["beta_step"], 2)
            dve.tensor_copy(sb["beta"][:, :].rearrange("p (h c) -> p h c", c=NCH),
                            beta_tmp.rearrange("p (c h) -> p h c", h=HEADS)).then_inc(sem["beta_step"], 1)
            dve.wait_ge(sem["down_loaded"], 16)
            for n in range(3):
                s = 256 << n
                a = wd[n % 2][:, :].rearrange("p (n two s) -> p n two s", two=2, s=s)
                b = wd[(n + 1) % 2][:, :].rearrange("p (n two s) -> p n two s", two=2, s=s)
                wait(dve, sem["w_mixed"], 2 * n)
                for half, op in enumerate((ALU.add, ALU.subtract)):
                    dve.tensor_tensor(b[:, :, half, :], a[:, :, 0, :], a[:, :, 1, :], op).then_inc(sem["w_mixed"], 1)
            dve.wait_ge(sem["w_had"], 1)
            dve.wait_ge(sem["wdp_scaled"], 1)
            for f in range(FT):
                dve.scalar_tensor_tensor(wd[0][:, D * f:D * f + D], ps[:, 2048 + D * f:2048 + D * f + D],
                                         su_dp[:, f:f + 1], wdp32, ALU.mult, ALU.mult).then_inc(sem["w_down_ready"], 1)
            for f in range(FT):
                dve.wait_ge(sem["silu"], f + 1)
                dve.scalar_tensor_tensor(y[:, f, :], ps[:, 2048 * (f % 2) + 1024:2048 * (f % 2) + 2048],
                                         wsc16[:, f:f + 1], silu_t[f % 2][:, :], ALU.mult, ALU.mult)\
                   .then_inc(sem["y_ready"], 1)
            for g in range(NCH // 2):
                dve.wait_ge(sem["down"], g + 1)
                dve.tensor_tensor(acc[:, 2 * g:2 * g + 2, :], acc[:, 2 * g:2 * g + 2, :],
                                  ps[:, 512 * g:512 * g + 512].rearrange("p (c d) -> p c d", c=2), ALU.add)\
                   .then_inc(sem["acc_ready"], 1)
            dve.wait_ge(sem["acc_ready"], NCH // 2)
            dve.wait_ge(sem["beta_step"], 3)
            dve.wait_ge(sem["hw_ready"], 1)

        @block.tensor
        def _(pe):
            pe.wait_ge(sem["const_loaded"], 32)
            for c in range(NCH):
                pe.wait_ge(sem["xn"], c + 1)
                for k in range(KT):
                    last = pe.transpose(ps[:, 512 * c + P * k:512 * c + P * (k + 1)],
                                        xn_tile(c)[:, P * k:P * (k + 1)], ident)
                last.then_inc(sem["xn_T"], 1)
            pe.wait_ge(sem["xn_T_copied"], NCH)
            pe.wait_ge(sem["small_w_loaded"], 16)
            for n, w in enumerate((f_w1, g_w1)):
                for b in range(BATCH):
                    for k in range(KT):
                        last = pe.matmul(ps[:, 1024 * n + SEQ * b:1024 * n + SEQ * (b + 1)], w[:, k, :],
                                         xnT[:, k, SEQ * b:SEQ * (b + 1)], start=(k == 0), stop=(k == KT - 1))
                last.then_inc(sem["shared"], 1)
            for c in range(NCH):
                for k in range(KT):
                    last = pe.matmul(ps[:, 2048 + HEADS * c:2048 + HEADS * (c + 1)], xnT[:, k, c * P:(c + 1) * P],
                                     b_w[:, k, :], start=(k == 0), stop=(k == KT - 1))
            last.then_inc(sem["shared"], 1)
            for k in range(KT):
                pe.wait_ge(sem["x_mixed"], k + 1)
                pe.wait_ge(sem["shared_copied"], k + 1)
                for b in range(BATCH):
                    last = pe.matmul(ps[:, 1024 * k + SEQ * b:1024 * k + SEQ * (b + 1)], hadamard,
                                     mixed[k][:, SEQ * b:SEQ * (b + 1)], start=True, stop=True)
                last.then_inc(sem["x_had"], 1)
            pe.wait_ge(sem["w_mixed"], 6)
            pe.wait_ge(sem["beta_exp"], 1)
            for n in range(4):
                last = pe.matmul(ps[:, 2048 + 512 * n:2048 + 512 * (n + 1)], hadamard,
                                 wd[1][:, 512 * n:512 * (n + 1)], start=True, stop=True)
            last.then_inc(sem["w_had"], 1)
            pe.wait_ge(sem["x_had_copied"], KT)
            pe.wait_ge(sem["gate_loaded"], 16)
            pe.wait_ge(sem["up_loaded"], 16)
            for f in range(FT):
                if f == 1:
                    pe.wait_ge(sem["w_down_ready"], FT)
                if f >= 2:
                    pe.wait_ge(sem["y_ready"], f - 1)
                for n, w in enumerate((w_gate, w_up)):
                    at = 2048 * (f % 2) + 1024 * n
                    for b in range(BATCH):
                        for k in range(KT):
                            last = pe.matmul(ps[:, at + SEQ * b:at + SEQ * (b + 1)], w[:, k, P * f:P * (f + 1)],
                                             x_had[:, k, SEQ * b:SEQ * (b + 1)], start=(k == 0), stop=(k == KT - 1))
                last.then_inc(sem["gate_up"], 1)
            pe.wait_ge(sem["y_ready"], FT)
            for g in range(NCH // 2):
                for c in (2 * g, 2 * g + 1):
                    for f in range(FT):
                        last = pe.matmul(ps[:, D * c:D * (c + 1)], y[:, f, c * P:(c + 1) * P],
                                         wd[0][:, D * f:D * (f + 1)], start=(f == 0), stop=(f == FT - 1))
                last.then_inc(sem["down"], 1)


def heads_block(nc, io, sb, ps, names):
    def new(*ns):
        for n in ns:
            sem[n] = names.enter_context(nc.semaphore(n))
    sem = {}
    new("a_rows_loaded0", "a_rows_loaded1", "b_rows_loaded0", "b_rows_loaded1", "c_rows_loaded0", "c_rows_loaded1",
        "zeroed", "stored")
    new("q_proj", "k_proj", "v_proj", "gate_proj", "g_proj", "ssq_ready", "ssk_ready", "vT_ready", "oT_ready",
        "out_ready", "scores_ready", "x_ready", "t_ready", "p1_ready", "u_ready", "o_ready", "ds_ready")
    new("pj_free", "sc_free")
    new("q_tap0", "k_tap0", "v_tap0", "q_silu", "k_silu", "v_silu", "q_sq", "k_sq", "gate_tanh", "z_abs", "z_exp",
        "z_ln", "a_ready", "a_scale", "xb_ready", "ub_ready", "o_copied", "o_sq", "khat_ready")
    new("q_taps", "k_taps", "v_taps", "at_ready", "aq_ready", "t_updated", "rhs_ready", "s_ready", "ssq_step",
        "ssk_step", "rq_ready", "c_ready", "gate_ready", "z_relu", "z_w", "z_step", "vn_ready", "norm_step",
        "on_ready", "ot_gated", "acc_added")
    new("scaled", "t_init", "rq_root", "nk_root", "norm_root")

    cst, beta, hw = sb["cst"], sb["beta"], sb["hw"]
    ident = cst[:, P:2 * P]
    masks = [cst[:, 2 * P + 64 * l:2 * P + 64 * (l + 1)] for l in range(LEVELS)]
    xnT, f1T, g1T, acc = sb["xnT"], sb["f1T"], sb["g1T"], sb["acc"]
    k_s, kq, aq, r_t, k_hat, vn, g_sig = (sb[n] for n in ("k", "kq", "aq", "r_t", "k_hat", "vn", "g_sig"))
    q_s, a_s, v_s, tot, t_s, o_raw, oT = (sb[n] for n in ("q", "a", "v", "tot", "t_s", "o_raw", "oT"))
    d = sb["d"]
    state, rhs, u_s = sb["state"], sb["rhs"], sb["u"]
    wa, wb, wc = sb["wa"], sb["wb"], sb["wc"]
    tiny = sb["tiny"]
    nk = [tiny[:, 64 * n:64 * n + 8] for n in range(2)]
    cc_ = [tiny[:, 64 * n + 8:64 * n + 16] for n in range(2)]
    rq = [tiny[:, 64 * n + 16:64 * n + 24] for n in range(2)]
    rqd = [tiny[:, 64 * n + 24:64 * n + 32] for n in range(2)]
    rq2 = [tiny[:, 64 * n + 32:64 * n + 40] for n in range(2)]
    totc = [tiny[:, 64 * n + 40:64 * n + 48] for n in range(2)]
    ci = [tiny[:, 64 * n + 48:64 * n + 56] for n in range(2)]
    ssq_e, ssk_e = tiny[:, 162:170], tiny[:, 170:178]
    inv_root, root = sb["powers"][:, 0:NCH], sb["powers"][:, NCH:2 * NCH]
    sso, ms, rr, rs = (tiny[:, 128 + 8 * n:136 + 8 * n] for n in range(4))
    a_scale, half_gb = tiny[:, 160:161], tiny[:, 161:162]
    at_b = [sb["lv"][:, 1024 * l:1024 * (l + 1)].rearrange("p (c i) -> p c i", c=NCH) for l in range(LEVELS)]
    x_b = [sb["lv"][:, 1024 * (LEVELS + l):1024 * (LEVELS + l + 1)].rearrange("p (c i) -> p c i", c=NCH)
           for l in range(LEVELS)]

    pj, sc = ps[:, 0:1024], ps[:, 1024:2048]
    x_p = tu_p = ps[:, 2048:2560]
    ru_p = ps[:, 2560:3072]
    seq_a, seq_b = ps[:, 3072:3328], ps[:, 3584:3840]

    def by_chunk(ap):
        return ap.rearrange("p (c i) -> p c i", c=NCH)

    def halves(ap, l, half):
        return ap.rearrange("p (n two s) -> p n two s", two=2, s=1 << l)[:, :, half, :]

    def chunk_halves(ap, l, half):
        return ap.rearrange("p c (n two s) -> p c n two s", two=2, s=1 << l)[:, :, :, half, :]

    def packed(ap, l):
        return ap.rearrange("p c (n s) -> p c n s", s=1 << l)

    def tot_at(l):
        if l == 0:
            return a_s[:, :]
        at = 1024 - (2048 >> l)
        return tot[:, at:at + (1024 >> l)]

    def each(ap):
        return ap.unsqueeze(2).broadcast_to([P, NCH, P])

    def pj_before(i, n):
        if isinstance(i, int):
            if i == -1:
                return n
            if i == 0:
                return PJ_PREP + n
            if i == HEADS:
                return pj_before(HEADS - 1, 0) + PJ_LEVEL + PJ_SCAN + n
        full = PJ_PREP + PJ_LEVEL + PJ_SCAN
        return (i - 1) * full + (2 * PJ_PREP + PJ_LEVEL + n)

    def iterations(eng, body):
        body(-1, (0, 0), None, None)
        body(0, (0, 1), (0, 0), None)
        with eng.Fori(0, HEADS // 2 - 1) as g:
            body(2 * g + 1, (g + 1, 0), (g, 1), (g, 0))
            body(2 * g + 2, (g + 1, 1), (g + 1, 0), (g, 1))
        body(HEADS - 1, None, (HEADS // 2 - 1, 1), (HEADS // 2 - 1, 0))
        body(HEADS, None, None, (HEADS // 2 - 1, 1))

    def num(head):
        return 2 * head[0] + head[1]

    with nc.Block() as block:
        @block.sync
        def _(sp):
            def loads(i, b, m, s):
                def known(value):
                    return value if isinstance(value, int) else sp.snap(value)

                def counts(h):
                    return bass.ds(known(h * P), P), known(h - 1), h
                ready_b = counts(num(b)) if b else None
                ready_m = counts(num(m)) if m else None
                if b:
                    at, used, h = ready_b
                    wait(sp, sem["a_scale"], used)
                    wait(sp, sem["g_proj"], used)
                    wait(sp, sem["k_silu"], used)
                    wait(sp, sem["z_relu"], used)
                    sp.dma_start(wa[b[1]][:, :], io["rows_a"][at, :]).then_inc(sem[f"a_rows_loaded{b[1]}"], 16)
                if m:
                    at, used, h = ready_m
                    wait(sp, sem["gate_ready"], used)
                    wait(sp, sem["v_silu"], used)
                    sp.dma_start(wb[m[1]][:, :], io["rows_b"][at, :]).then_inc(sem[f"b_rows_loaded{m[1]}"], 16)
                    wait(sp, sem["khat_ready"], h)
                    sp.dma_start(wc[m[1]][:, :], io["o_w"][at, :]).then_inc(sem[f"c_rows_loaded{m[1]}"], 16)

            iterations(sp, loads)
            sp.wait_ge(sem["acc_added"], 2 * HEADS)
            for c in range(NCH):
                sp.dma_start(io["out"][c * P:(c + 1) * P, :], acc[:, c, :]).then_inc(sem["stored"], 16)
            sp.wait_ge(sem["stored"], 16 * NCH)

        @block.gpsimd
        def _(pool):
            for l in range(LEVELS):
                pool.memset(at_b[l], 0.0).then_inc(sem["zeroed"], 1)
                pool.memset(x_b[l], 0.0).then_inc(sem["zeroed"], 1)

            def query_root(b):
                pool.wait_ge(sem["ssq_step"], num(b) + 1)
                wait(pool, sem["rq_ready"], 2 * (num(b) - 1))
                pool.tensor_tensor(rq[b[1]], ssq_e, inv_root, ALU.pow).then_inc(sem["rq_root"], 1)

            def key_root(b):
                pool.wait_ge(sem["ssk_step"], 2 * num(b) + 1)
                wait(pool, sem["vn_ready"], num(b) - 1)
                pool.tensor_tensor(nk[b[1]], ssk_e, root, ALU.pow).then_inc(sem["nk_root"], 1)

            def output_root(s):
                pool.wait_ge(sem["norm_step"], 4 * num(s) + 3)
                pool.tensor_tensor(rr, ms, inv_root, ALU.pow).then_inc(sem["norm_root"], 1)

            def level_scales(i, b, m, s):
                if not m:
                    if b:
                        query_root(b)
                        key_root(b)
                    if s:
                        output_root(s)
                    return
                h, p = num(m), m[1]
                done = 23 * h
                kk, qq = kq[p][:, 0:1024], kq[p][:, 1024:2048]
                wait(pool, sem["o_ready"], 4 * (h - 1))
                wait(pool, sem["p1_ready"], 3 * (h - 1))
                wait(pool, sem["k_silu"], h + 1)
                wait(pool, sem["q_silu"], h + 1)
                wait(pool, sem["a_ready"], h + 1)
                pool.tensor_tensor(kk, k_s[p][:, :], a_s[:, :], ALU.mult).then_inc(sem["scaled"], 1)
                pool.tensor_tensor(qq, q_s[:, :], a_s[:, :], ALU.mult).then_inc(sem["scaled"], 1)
                wait(pool, sem["c_ready"], h + 1)
                wait(pool, sem["t_ready"], LEVELS * h)
                ident_b = ident.unsqueeze(1).broadcast_to([P, NCH, P])
                pool.tensor_tensor(by_chunk(t_s[:, :]), ident_b, each(cc_[p]), ALU.mult).then_inc(sem["t_init"], 1)
                wait(pool, sem["u_ready"], 4 * (h - 1))
                pool.tensor_tensor(by_chunk(r_t[p][:, :]), ident_b, each(cc_[p]), ALU.mult).then_inc(sem["t_init"], 1)
                for l in range(1, LEVELS + 1):
                    before = tot_at(l - 1).rearrange("p (n two) -> p n two", two=2)
                    n = 1024 >> l
                    if l == 4 and b:
                        query_root(b)
                    if l == 5 and b:
                        key_root(b)
                    if l == 5 and s:
                        output_root(s)
                    pool.wait_ge(sem["scores_ready"], SC_PER_HEAD * h + l + 1)
                    if l == 1:
                        pool.wait_ge(sem["k_sq"], h + 1)
                    pool.wait_ge(sem["scaled"], done + scaled_count(l - 1))
                    both = kq[p][:, :].rearrange("p (w n two s) -> p w n two s", w=2, two=2, s=1 << (l - 1))[:, :, :, 1, :]
                    pool.tensor_tensor(both, both, before[:, :, 0].unsqueeze(1).unsqueeze(3)
                                       .broadcast_to([P, 2, n, 1 << (l - 1)]), ALU.mult).then_inc(sem["scaled"], 1)
                    first = halves(k_s[p][:, :], l - 1, 0)
                    pool.tensor_tensor(first, first, before[:, :, 1].unsqueeze(2)
                                       .broadcast_to([P, n, 1 << (l - 1)]), ALU.mult).then_inc(sem["scaled"], 1)
                    if l == LEVELS:
                        wait(pool, sem["s_ready"], 5 * (h - 1))
                    after = totc[p] if l == LEVELS else tot_at(l)
                    pool.tensor_tensor(after, before[:, :, 0], before[:, :, 1], ALU.mult).then_inc(sem["scaled"], 1)

            iterations(pool, level_scales)

        @block.tensor
        def _(pe):
            def body(i, b, m, s):
                use = [0]

                def take_pj():
                    wait(pe, sem["pj_free"], pj_before(i, use[0]))
                    use[0] += 1

                def project(w, src, kts, done):
                    for n in range(BATCH):
                        for k in range(kts):
                            last = pe.matmul(pj[:, SEQ * n:SEQ * (n + 1)], w[:, P * k:P * (k + 1)],
                                             src[:, k, SEQ * n:SEQ * (n + 1)] if kts > 1
                                             else src[:, SEQ * n:SEQ * (n + 1)],
                                             start=(k == 0), stop=(k == kts - 1))
                    last.then_inc(done, 1)

                def scores(l):
                    h, p = num(m), m[1]
                    if l < 0:
                        pe.wait_ge(sem["k_silu"], h + 1)
                        pe.wait_ge(sem["q_silu"], h + 1)
                    else:
                        pe.wait_ge(sem["scaled"], 23 * h + scaled_count(l))
                    wait(pe, sem["sc_free"], SC_PER_HEAD * h + l + 1)
                    for c in range(NCH):
                        key = k_s[p][:, c * P:(c + 1) * P]
                        if l < 0:
                            moving = q_s[:, c * P:(c + 1) * P]
                        else:
                            moving = kq[p][:, :].rearrange("p (w c i) -> p w c i", w=2, c=NCH)[:, :, c, :]\
                                .rearrange("p w (n two s) -> p w n two s", two=2, s=1 << l)[:, :, :, 1, :]
                        last = pe.matmul(sc[:, c * P:(c + 1) * P], key, moving, start=True, stop=True)
                    last.then_inc(sem["scores_ready"], 1)

                def x_product(l):
                    h, p = num(m), m[1]
                    pe.wait_ge(sem["at_ready"], LEVELS * h + l + 1)
                    if l == 0:
                        pe.wait_ge(sem["t_init"], 2 * h + 2)
                    wait(pe, sem["t_updated"], 13 * h + 2 * l)
                    wait(pe, sem["xb_ready"], LEVELS * h + l)
                    for c in range(NCH):
                        last = pe.matmul(x_p[:, 64 * c:64 * (c + 1)], at_b[l][:, c, :],
                                         halves(t_s[:, c * P:(c + 1) * P], l, 0), start=True, stop=True)
                    last.then_inc(sem["x_ready"], 1)

                def t_product(l):
                    h, p = num(m), m[1]
                    pe.wait_ge(sem["xb_ready"], LEVELS * h + l + 1)
                    wait(pe, sem["t_updated"], 13 * h + 2 * l)
                    for c in range(NCH):
                        rt = r_t[p][:, c * P:(c + 1) * P]
                        if l < LEVELS - 1:
                            pe.matmul(tu_p[:, 64 * c:64 * (c + 1)], rt, halves(x_b[l][:, c, :], l, 0),
                                      start=True, stop=True)
                        last = pe.matmul(ru_p[:, 64 * c:64 * (c + 1)], x_b[l][:, c, :], halves(rt, l, 1),
                                         start=True, stop=True)
                    last.then_inc(sem["t_ready"], 1)

                def scan_state(c):
                    if c == 0:
                        return
                    h, p = num(s), s[1]
                    pe.wait_ge(sem["s_ready"], 5 * h + 2 * c - 1)
                    for n in range(BATCH):
                        at = (n * CPB + c) * P
                        last = pe.matmul(seq_a[:, n * P:(n + 1) * P], kq[p][:, at:at + P],
                                         state[c % 2][:, n * P:(n + 1) * P], start=True, stop=True)
                    last.then_inc(sem["p1_ready"], 1)

                def scan_u(c):
                    h, p = num(s), s[1]
                    if c == 0:
                        pe.wait_ge(sem["vn_ready"], h + 1)
                        pe.wait_ge(sem["t_updated"], 13 * (h + 1))
                    else:
                        pe.wait_ge(sem["rhs_ready"], 3 * h + c)
                    wait(pe, sem["o_copied"], 4 * h + c)
                    for n in range(BATCH):
                        cc = n * CPB + c
                        r = vn[p][:, cc * P:(cc + 1) * P] if c == 0 else rhs[:, n * P:(n + 1) * P]
                        last = pe.matmul(seq_b[:, n * P:(n + 1) * P], r_t[p][:, cc * P:(cc + 1) * P], r,
                                         start=True, stop=True)
                    last.then_inc(sem["u_ready"], 1)

                def scan_out(c):
                    h, p = num(s), s[1]
                    pe.wait_ge(sem["ub_ready"], 4 * h + c + 1)
                    if c == 0:
                        pe.wait_ge(sem["khat_ready"], h + 1)
                        pe.wait_ge(sem["aq_ready"], (LEVELS + 1) * (h + 1))
                    if c < CPB - 1:
                        for n in range(BATCH):
                            cc = n * CPB + c
                            last = pe.matmul(seq_a[:, n * P:(n + 1) * P], k_hat[p][:, cc * P:(cc + 1) * P],
                                             u_s[:, n * P:(n + 1) * P], start=True, stop=True)
                        last.then_inc(sem["ds_ready"], 1)
                    for n in range(BATCH):
                        cc = n * CPB + c
                        last = pe.matmul(seq_b[:, n * P:(n + 1) * P], aq[p][:, cc * P:(cc + 1) * P],
                                         u_s[:, n * P:(n + 1) * P], start=True, stop=(c == 0))
                        if c > 0:
                            last = pe.matmul(seq_b[:, n * P:(n + 1) * P],
                                             kq[p][:, 1024 + cc * P:1024 + (cc + 1) * P],
                                             state[c % 2][:, n * P:(n + 1) * P], start=False, stop=True)
                    last.then_inc(sem["o_ready"], 1)

                def sums_of_squares(done):
                    for c in range(NCH):
                        last = pe.matmul(pj[:, c:c + 1], d[3][:, c * P:(c + 1) * P], sb["ones"][:, 0:1],
                                         start=True, stop=True)
                    last.then_inc(done, 1)

                def turn(src, dst, done):
                    for c in range(NCH):
                        last = pe.transpose(dst[:, c * P:(c + 1) * P], src[:, c * P:(c + 1) * P], ident)
                    last.then_inc(done, 1)

                def out_product(half):
                    h, p = num(s), s[1]
                    take_pj()
                    if half == 0:
                        pe.wait_ge(sem["ot_gated"], h + 1)
                        pe.wait_ge(sem[f"c_rows_loaded{p}"], 16 * (s[0] + 1))
                    for c in range(4):
                        cc = 4 * half + c
                        last = pe.matmul(pj[:, D * c:D * (c + 1)], oT[:, cc * P:(cc + 1) * P], wc[p][:, :],
                                         start=True, stop=True)
                    last.then_inc(sem["out_ready"], 1)

                if m:
                    scores(-1)
                for l in range(LEVELS):
                    if m:
                        scores(l)
                    if s and l < CPB:
                        scan_state(l)
                    if l == 0 and b:
                        pe.wait_ge(sem[f"a_rows_loaded{b[1]}"], 16 * (b[0] + 1))
                        take_pj()
                        project(wa[b[1]][:, A_Q:], xnT, KT, sem["q_proj"])
                    if l == 1 and b:
                        take_pj()
                        project(wa[b[1]][:, A_K:], xnT, KT, sem["k_proj"])
                    if l == 2 and m:
                        pe.wait_ge(sem[f"b_rows_loaded{m[1]}"], 16 * (m[0] + 1))
                        take_pj()
                        project(wb[m[1]][:, B_V:], xnT, KT, sem["v_proj"])
                    if l == 3 and m:
                        take_pj()
                        project(wb[m[1]][:, B_G2:], g1T, 1, sem["gate_proj"])
                    if l == 4 and b:
                        take_pj()
                        project(wa[b[1]][:, A_F2:], f1T, 1, sem["g_proj"])
                    if l == 5 and s:
                        take_pj()
                        pe.wait_ge(sem["on_ready"], num(s) + 1)
                        turn(o_raw, pj, sem["oT_ready"])
                    if l == 6 and s:
                        out_product(0)
                    if m:
                        x_product(l)
                    if s and l < CPB:
                        scan_u(l)
                    if m:
                        t_product(l)
                    if s and l < CPB:
                        scan_out(l)
                    if l == 2 and b:
                        take_pj()
                        pe.wait_ge(sem["q_sq"], num(b) + 1)
                        sums_of_squares(sem["ssq_ready"])
                    if l == 3 and b:
                        take_pj()
                        pe.wait_ge(sem["k_sq"], num(b) + 1)
                        sums_of_squares(sem["ssk_ready"])
                    if l == 5 and m:
                        take_pj()
                        pe.wait_ge(sem["v_silu"], num(m) + 1)
                        turn(v_s, pj, sem["vT_ready"])
                    if l == 6 and s:
                        out_product(1)
                if m:
                    h = num(m)
                    pe.wait_ge(sem["scaled"], 23 * (h + 1))
                    pe.wait_ge(sem["sc_free"], SC_PER_HEAD * h + LEVELS + 1)
                    turn(k_s[m[1]], sc, sem["scores_ready"])

            iterations(pe, body)

        @block.scalar
        def _(act):
            def body(i, b, m, s):
                hb, hm, hs = (num(x) if x else None for x in (b, m, s))

                def tap0(name, dst, w, h):
                    act.wait_ge(sem[name + "_proj"], h + 1)
                    act.activation(dst[:, :], pj, ACT.Copy, scale=w).then_inc(sem[name + "_tap0"], 1)

                def silu(name, buf, h):
                    act.wait_ge(sem[name + "_taps"], 3 * (h + 1))
                    act.activation(buf[:, :], buf[:, :], ACT.Silu).then_inc(sem[name + "_silu"], 1)

                for l in range(LEVELS):
                    if l == 0 and b:
                        wait(act, sem["scaled"], 23 * (hb - 1) + 2)
                        wait(act, sem["scores_ready"], SC_PER_HEAD * (hb - 1) + 1)
                        wait(act, sem["q_sq"], hb)
                        act.wait_ge(sem[f"a_rows_loaded{b[1]}"], 16 * (b[0] + 1))
                        tap0("q", q_s, wa[b[1]][:, A_C + 3:A_C + 4], hb)
                    if l == 1 and b:
                        wait(act, sem["scores_ready"], SC_PER_HEAD * (hb - 1))
                        tap0("k", k_s[b[1]], wa[b[1]][:, A_C + 7:A_C + 8], hb)
                    if l == 2 and m:
                        wait(act, sem["vT_ready"], hm)
                        act.wait_ge(sem[f"b_rows_loaded{m[1]}"], 16 * (m[0] + 1))
                        tap0("v", v_s, wb[m[1]][:, B_C + 3:B_C + 4], hm)
                    if m:
                        act.wait_ge(sem["x_ready"], LEVELS * hm + l + 1)
                        if isinstance(hm, int) and hm == 0 and l == 0:
                            act.wait_ge(sem["zeroed"], 2 * LEVELS)
                        wait(act, sem["t_ready"], LEVELS * (hm - 1) + l + 1)
                        act.activation(chunk_halves(x_b[l], l, 0),
                                       packed(x_p.rearrange("p (c i) -> p c i", c=NCH), l), ACT.Copy)\
                           .then_inc(sem["xb_ready"], 1)
                    if s and l < CPB:
                        act.wait_ge(sem["u_ready"], 4 * hs + l + 1)
                        wait(act, sem["o_ready"], 4 * hs + l)
                        wait(act, sem["ds_ready"], 3 * hs + min(l, CPB - 1))
                        act.activation(u_s[:, :], seq_b, ACT.Copy).then_inc(sem["ub_ready"], 1)
                    if l == 1 and b:
                        silu("q", q_s, hb)
                        act.wait_ge(sem["q_silu"], hb + 1)
                        wait(act, sem["z_step"], 3 * hb)
                        act.activation(d[3][:, :], q_s[:, :], ACT.Square).then_inc(sem["q_sq"], 1)
                    if l == 2 and b:
                        silu("k", k_s[b[1]], hb)
                    if l == 3:
                        if m:
                            silu("v", v_s, hm)
                            act.wait_ge(sem["gate_proj"], hm + 1)
                            act.activation(half_gb, wb[m[1]][:, B_C + 4:B_C + 5], ACT.Copy, scale=0.5)\
                               .then_inc(sem["gate_tanh"], 1)
                            act.wait_ge(sem["gate_tanh"], 2 * hm + 1)
                            wait(act, sem["ot_gated"], hm - 1)
                            act.activation(g_sig[m[1]][:, :], pj, ACT.Tanh, bias=half_gb, scale=0.5)\
                               .then_inc(sem["gate_tanh"], 1)
                            act.wait_ge(sem["gate_tanh"], 2 * hm + 2)
                            act.sem_inc(sem["pj_free"], 1)
                        if b:
                            act.wait_ge(sem["k_silu"], hb + 1)
                            act.wait_ge(sem["ssq_ready"], hb + 1)
                            act.activation(d[3][:, :], k_s[b[1]][:, :], ACT.Square).then_inc(sem["k_sq"], 1)
                    if s and l < CPB:
                        act.wait_ge(sem["o_ready"], 4 * hs + l + 1)
                        if l == 0:
                            wait(act, sem["oT_ready"], hs)
                        act.activation(o_raw[:, :].rearrange("p (b c v) -> p b c v", b=BATCH, c=CPB)[:, :, l, :],
                                       seq_b.rearrange("p (b v) -> p b v", b=BATCH), ACT.Copy)\
                           .then_inc(sem["o_copied"], 1)
                    if l == 3 and s:
                        act.wait_ge(sem["o_copied"], 4 * hs + 4)
                        wait(act, sem["out_ready"], 2 * hs)
                        act.activation(oT[:, :], o_raw[:, :], ACT.Square).then_inc(sem["o_sq"], 1)
                    if l == 4 and b:
                        w = wa[b[1]]
                        wait(act, sem["a_ready"], hb)
                        act.activation(a_scale, w[:, A_C + 9:A_C + 10], ACT.Exp).then_inc(sem["a_scale"], 1)
                        act.wait_ge(sem["g_proj"], hb + 1)
                        wait(act, sem["z_step"], 3 * hb)
                        act.activation(d[0][:, :], pj, ACT.Abs, bias=w[:, A_C + 8:A_C + 9]).then_inc(sem["z_abs"], 1)
                        act.wait_ge(sem["z_abs"], hb + 1)
                        act.activation(d[1][:, :], d[0][:, :], ACT.Exp, scale=-1.0).then_inc(sem["z_exp"], 1)
                    if l == 5 and b:
                        act.wait_ge(sem["z_w"], hb + 1)
                        act.wait_ge(sem["ssk_ready"], hb + 1)
                        act.activation(d[3][:, :], d[0][:, :], ACT.Ln).then_inc(sem["z_ln"], 1)
                    if l == 6 and b:
                        act.wait_ge(sem["z_step"], 3 * hb + 3)
                        wait(act, sem["scaled"], 23 * (hb - 1) + scaled_count(1))
                        act.wait_ge(sem["a_scale"], hb + 1)
                        act.activation(a_s[:, :], d[1][:, :], ACT.Exp, scale=a_scale).then_inc(sem["a_ready"], 1)
                if m:
                    act.wait_ge(sem["scores_ready"], SC_PER_HEAD * (hm + 1))
                    wait(act, sem["ds_ready"], 3 * (hm - 1))
                    act.activation(k_hat[m[1]][:, :], sc, ACT.Copy).then_inc(sem["khat_ready"], 1)
                    act.wait_ge(sem["khat_ready"], hm + 1)
                    act.sem_inc(sem["sc_free"], 1)

            iterations(act, body)

        @block.vector
        def _(dve):
            def body(i, b, m, s):
                hb, hm, hs = (num(x) if x else None for x in (b, m, s))

                def tap(name, dst, w, at, h, n):
                    if n == 1:
                        dve.wait_ge(sem[name + "_tap0"], h + 1)
                    else:
                        dve.wait_ge(sem[name + "_taps"], 3 * h + n - 1)
                    y = dst[:, :].rearrange("p (b t) -> p b t", b=BATCH)[:, :, n:]
                    x = pj.rearrange("p (b t) -> p b t", b=BATCH)[:, :, 0:SEQ - n]
                    dve.scalar_tensor_tensor(y, x, w[:, at + TAPS - 1 - n:at + TAPS - n], y, ALU.mult, ALU.add)\
                       .then_inc(sem[name + "_taps"], 1)
                    if n == TAPS - 1:
                        dve.wait_ge(sem[name + "_taps"], 3 * h + 3)
                        dve.sem_inc(sem["pj_free"], 1)

                def conv(l, ns):
                    if l == 0 and b:
                        for n in ns:
                            tap("q", q_s, wa[b[1]], A_C, hb, n)
                    if l == 1 and b:
                        for n in ns:
                            tap("k", k_s[b[1]], wa[b[1]], A_C + 4, hb, n)
                    if l == 2 and m:
                        for n in ns:
                            tap("v", v_s, wb[m[1]], B_C, hm, n)

                def add_out(half):
                    dve.wait_ge(sem["out_ready"], 2 * hs + half + 1)
                    a = acc[:, 4 * half:4 * half + 4, :]
                    dve.tensor_tensor(a, a, pj.rearrange("p (c d) -> p c d", c=4), ALU.add)\
                       .then_inc(sem["acc_added"], 1)
                    dve.wait_ge(sem["acc_added"], 2 * hs + half + 1)
                    dve.sem_inc(sem["pj_free"], 1)

                if m:
                    p = m[1]
                    dve.wait_ge(sem["rq_root"], hm + 1)
                    wait(dve, sem["norm_step"], 4 * (hm - 1))
                    dve.tensor_scalar(rqd[p], rq[p], float(P) ** -0.5, None, ALU.mult).then_inc(sem["rq_ready"], 1)
                    dve.wait_ge(sem["rq_ready"], 2 * hm + 1)
                    dve.scalar_tensor_tensor(rq2[p], rqd[p], 1.0 / P, rqd[p], ALU.mult, ALU.mult)\
                       .then_inc(sem["rq_ready"], 1)
                    dve.wait_ge(sem["scores_ready"], SC_PER_HEAD * hm + 1)
                    wait(dve, sem["o_ready"], 4 * (hm - 1))
                    dve.tensor_tensor(by_chunk(aq[p][:, :]), by_chunk(sc),
                                      ident.unsqueeze(1).broadcast_to([P, NCH, P]), ALU.mult)\
                       .then_inc(sem["aq_ready"], 1)
                    dve.wait_ge(sem["aq_ready"], (LEVELS + 1) * hm + 1)
                    dve.sem_inc(sem["sc_free"], 1)
                for l in range(LEVELS):
                    if m:
                        p = m[1]
                        mask = masks[l].unsqueeze(1).broadcast_to([P, NCH, 64])
                        keys, queries = by_chunk(sc)[:, :, 0:64], by_chunk(sc)[:, :, 64:128]
                        dve.wait_ge(sem["scores_ready"], SC_PER_HEAD * hm + l + 2)
                        if isinstance(hm, int) and hm == 0 and l == 0:
                            dve.wait_ge(sem["zeroed"], 2 * LEVELS)
                        dve.wait_ge(sem["aq_ready"], (LEVELS + 1) * hm + l + 1)
                        wait(dve, sem["x_ready"], LEVELS * (hm - 1) + l + 1)
                        dve.tensor_tensor(chunk_halves(at_b[l], l, 1), packed(keys, l), packed(mask, l), ALU.mult)\
                           .then_inc(sem["at_ready"], 1)
                        dve.copy_predicated(chunk_halves(by_chunk(aq[p][:, :]), l, 1), packed(mask.bitcast(U32), l),
                                            packed(queries, l)).then_inc(sem["aq_ready"], 1)
                        dve.wait_ge(sem["at_ready"], LEVELS * hm + l + 1)
                        dve.wait_ge(sem["aq_ready"], (LEVELS + 1) * hm + l + 2)
                        dve.sem_inc(sem["sc_free"], 1)
                    if s and 1 <= l < CPB:
                        dve.wait_ge(sem["p1_ready"], 3 * hs + l)
                        wait(dve, sem["u_ready"], 4 * hs + l)
                        dve.tensor_tensor(rhs[:, :].rearrange("p (b v) -> p b v", b=BATCH),
                                          vn[s[1]][:, :].rearrange("p (b c v) -> p b c v", b=BATCH, c=CPB)[:, :, l, :],
                                          seq_a.rearrange("p (b v) -> p b v", b=BATCH), ALU.subtract)\
                           .then_inc(sem["rhs_ready"], 1)
                    conv(l, (1, 2))
                    if l == 4 and s:
                        p = s[1]
                        dve.wait_ge(sem["o_sq"], hs + 1)
                        dve.tensor_reduce(sso, by_chunk(oT[:, :]), AX_X, ALU.add).then_inc(sem["norm_step"], 1)
                        dve.wait_ge(sem["norm_step"], 4 * hs + 1)
                        dve.wait_ge(sem["rq_ready"], 2 * hs + 2)
                        dve.tensor_tensor(ms, sso, rq2[p], ALU.mult).then_inc(sem["norm_step"], 1)
                        dve.wait_ge(sem["norm_step"], 4 * hs + 2)
                        wait(dve, sem["norm_root"], hs)
                        dve.tensor_scalar(ms, ms, EPS_NORM, None, ALU.add).then_inc(sem["norm_step"], 1)
                    if l == 4 and b:
                        dve.wait_ge(sem["z_abs"], hb + 1)
                        dve.tensor_scalar(d[2][:, :], pj, wa[b[1]][:, A_C + 8:A_C + 9], 0.0, ALU.add, ALU.max)\
                           .then_inc(sem["z_relu"], 1)
                        dve.wait_ge(sem["z_relu"], hb + 1)
                        dve.sem_inc(sem["pj_free"], 1)
                    if l == 5 and s:
                        dve.wait_ge(sem["oT_ready"], hs + 1)
                        dve.wait_ge(sem["gate_ready"], hs + 1)
                        dve.tensor_tensor(oT[:, :], pj, g_sig[s[1]][:, :], ALU.mult).then_inc(sem["ot_gated"], 1)
                        dve.wait_ge(sem["ot_gated"], hs + 1)
                        dve.sem_inc(sem["pj_free"], 1)
                    if l == 6 and s:
                        add_out(0)
                    if m:
                        p = m[1]
                        dve.wait_ge(sem["t_ready"], LEVELS * hm + l + 1)
                        if l < LEVELS - 1:
                            t = chunk_halves(by_chunk(t_s[:, :]), l, 0)
                            dve.tensor_tensor(t, t, packed(tu_p.rearrange("p (c i) -> p c i", c=NCH), l),
                                              ALU.subtract).then_inc(sem["t_updated"], 1)
                        r = chunk_halves(by_chunk(r_t[p][:, :]), l, 1)
                        dve.tensor_tensor(r, r, packed(ru_p.rearrange("p (c i) -> p c i", c=NCH), l),
                                          ALU.subtract).then_inc(sem["t_updated"], 1)
                    if s and l < CPB - 1:
                        dve.wait_ge(sem["ds_ready"], 3 * hs + l + 1)
                        wait(dve, sem["o_ready"], 4 * hs + l)
                        nxt = state[(l + 1) % 2]
                        if l == 0:
                            dve.tensor_copy(nxt[:, :], seq_a).then_inc(sem["s_ready"], 1)
                        else:
                            for n in range(BATCH):
                                cc = n * CPB + l
                                dve.scalar_tensor_tensor(nxt[:, n * P:(n + 1) * P], state[l % 2][:, n * P:(n + 1) * P],
                                                         totc[s[1]][:, cc:cc + 1], seq_a[:, n * P:(n + 1) * P],
                                                         ALU.mult, ALU.add).then_inc(sem["s_ready"], 1)
                    conv(l, (3,))
                    if l == 4 and s:
                        dve.wait_ge(sem["norm_root"], hs + 1)
                        dve.tensor_tensor(rs, rr, rqd[s[1]], ALU.mult).then_inc(sem["norm_step"], 1)
                        dve.wait_ge(sem["norm_step"], 4 * hs + 4)
                        dve.tensor_tensor(by_chunk(o_raw[:, :]), by_chunk(o_raw[:, :]), each(rs), ALU.mult)\
                           .then_inc(sem["on_ready"], 1)
                    if l == 2 and b:
                        dve.wait_ge(sem["ssq_ready"], hb + 1)
                        wait(dve, sem["rq_root"], hb)
                        dve.tensor_scalar(ssq_e, pj[:, 0:NCH], EPS_L2, None, ALU.add)\
                           .then_inc(sem["ssq_step"], 1)
                        dve.wait_ge(sem["ssq_step"], hb + 1)
                        dve.sem_inc(sem["pj_free"], 1)
                    if l == 3 and m:
                        dve.wait_ge(sem["gate_tanh"], 2 * hm + 2)
                        dve.tensor_scalar(g_sig[m[1]][:, :], g_sig[m[1]][:, :], hw[:, 0:1], hw[:, 0:1], ALU.mult,
                                          ALU.add).then_inc(sem["gate_ready"], 1)
                    if l == 3 and b:
                        dve.wait_ge(sem["ssk_ready"], hb + 1)
                        wait(dve, sem["nk_root"], hb)
                        dve.tensor_scalar(ssk_e, pj[:, 0:NCH], EPS_L2, None, ALU.add)\
                           .then_inc(sem["ssk_step"], 1)
                        dve.wait_ge(sem["ssk_step"], 2 * hb + 1)
                        dve.sem_inc(sem["pj_free"], 1)
                        wait(dve, sem["t_init"], 2 * hb - 2)
                        dve.reciprocal(ci[b[1]], ssk_e).then_inc(sem["ssk_step"], 1)
                        dve.wait_ge(sem["ssk_step"], 2 * hb + 2)
                        dve.tensor_tensor(cc_[b[1]], ci[b[1]], beta[:, bass.ds(hb * NCH, NCH)], ALU.mult)\
                           .then_inc(sem["c_ready"], 1)
                    if l == 4 and b:
                        dve.wait_ge(sem["z_exp"], hb + 1)
                        dve.tensor_scalar(d[0][:, :], d[1][:, :], 1.0, None, ALU.add).then_inc(sem["z_w"], 1)
                    if l == 5 and b:
                        dve.wait_ge(sem["z_w"], hb + 1)
                        dve.scalar_tensor_tensor(d[1][:, :], d[0][:, :], 1.0, d[1][:, :], ALU.subtract, ALU.subtract)\
                           .then_inc(sem["z_step"], 1)
                    if l == 5 and m:
                        dve.wait_ge(sem["vT_ready"], hm + 1)
                        dve.wait_ge(sem["nk_root"], hm + 1)
                        wait(dve, sem["rhs_ready"], 3 * (hm - 1))
                        wait(dve, sem["u_ready"], 4 * (hm - 1))
                        dve.tensor_tensor(by_chunk(vn[m[1]][:, :]), by_chunk(pj), each(nk[m[1]]), ALU.mult)\
                           .then_inc(sem["vn_ready"], 1)
                        dve.wait_ge(sem["vn_ready"], hm + 1)
                        dve.sem_inc(sem["pj_free"], 1)
                    if l == 5 and b:
                        dve.wait_ge(sem["z_ln"], hb + 1)
                        dve.wait_ge(sem["z_step"], 3 * hb + 1)
                        dve.tensor_tensor(d[1][:, :], d[1][:, :], d[3][:, :], ALU.subtract).then_inc(sem["z_step"], 1)
                        dve.wait_ge(sem["z_step"], 3 * hb + 2)
                        dve.tensor_tensor(d[1][:, :], d[1][:, :], d[2][:, :], ALU.subtract).then_inc(sem["z_step"], 1)
                    if l == 6 and s:
                        add_out(1)

            iterations(dve, body)


def build(nc, io):
    with ExitStack() as ctx:
        def buf(name, cols):
            return ctx.enter_context(nc.sbuf_tensor(name, [P, cols], F32))

        def pair(name, cols):
            return [buf(f"{name}{n}", cols) for n in range(2)]

        sb = {
            "xnT": ctx.enter_context(nc.sbuf_tensor("xnT", [P, KT, TOK], F32)),
            "acc": ctx.enter_context(nc.sbuf_tensor("acc", [P, NCH, D], F32)),
            "f1T": buf("f1T", TOK), "g1T": buf("g1T", TOK),
            "lv": buf("level_matrices", 2 * LEVELS * TOK),
            "k": pair("k", TOK), "kq": pair("kq", 2 * TOK), "aq": pair("aq", TOK), "r_t": pair("r_t", TOK),
            "k_hat": pair("k_hat", TOK), "vn": pair("vn", TOK), "g_sig": pair("g_sig", TOK),
            "q": buf("q", TOK), "a": buf("a", TOK), "v": buf("v", TOK), "tot": buf("tot", TOK),
            "t_s": buf("t_s", TOK), "o_raw": buf("o_raw", TOK), "oT": buf("oT", TOK),
            "d": [buf(f"d{n}", TOK) for n in range(4)],
            "state": pair("state", BATCH * P), "rhs": buf("rhs", BATCH * P), "u": buf("u", BATCH * P),
            "wa": pair("wa", A_COLS), "wb": pair("wb", B_COLS), "wc": pair("wc", D),
            "cst": buf("cst", 2 * P + 64 * LEVELS), "beta": buf("beta", P), "hw": buf("hw", 1),
            "ones": buf("ones", 2), "tiny": buf("tiny", 178), "powers": buf("powers", 2 * NCH),
        }
        ps = ctx.enter_context(nc.psum_tensor("ps", [P, 4096], F32))
        fills_set = ctx.enter_context(nc.semaphore("fills_set"))
        nc.gpsimd.memset(sb["ones"][:, :], 1.0).then_inc(fills_set, 1)
        nc.gpsimd.memset(sb["powers"][:, 0:NCH], -0.5).then_inc(fills_set, 1)
        nc.gpsimd.memset(sb["powers"][:, NCH:2 * NCH], 0.5).then_inc(fills_set, 1)
        nc.gpsimd.wait_ge(fills_set, 3)
        setup_block(nc, io, sb, ps, ctx)
        heads_block(nc, io, sb, ps, ctx)


def shape_constants():
    h = np.ones((1, 1), np.float32)
    while h.shape[0] < P:
        h = np.block([[h, h], [h, -h]])
    cols = [h, np.eye(P, dtype=np.float32)]
    j = np.arange(P)[:, None]
    for l in range(LEVELS):
        i = np.array([n for n in range(P) if n >> l & 1])[None, :]
        cols.append(((j >> (l + 1) == i >> (l + 1)) & (j >> l & 1 == 0)).astype(np.float32))
    return np.ascontiguousarray(np.concatenate(cols, 1), np.float32)


def kernel(**inputs):
    import concourse.bacc as bacc
    from concourse.bass_utils import run_bass_kernel_spmd

    g = {n: np.asarray(v) for n, v in inputs.items()}
    at, ff = "L0_attn_", "L0_ffn_"

    def k_tiles(w):
        return w.reshape(KT, P, -1).transpose(1, 0, 2)

    def by_head(w):
        return w.reshape(KT, P, HEADS, P).transpose(2, 1, 0, 3).reshape(HEADS, P, KT * P)

    def rank(w):
        return w.reshape(P, HEADS, P).transpose(1, 0, 2)

    def per_channel(w):
        return w.reshape(HEADS, P, -1)

    def fill(n):
        return np.zeros((HEADS, P, n), np.float32)

    a_log = np.broadcast_to(g[at + "A_log"][:, None, None], (HEADS, P, 1))
    arrays = {
        "x": g[at + "hidden_states"].reshape(TOK, D),
        "consts": shape_constants(),
        "o_norm_w": g[at + "o_norm_w"].reshape(P, 1),
        "small_w": np.concatenate([k_tiles(g[at + n]).reshape(P, -1) for n in ("f_w1", "g_w1", "b_w")], 1),
        "ffn_consts": np.concatenate([
            g[ff + "SU_ug"].reshape(KT, P).T, g[ff + "SU_dp"].reshape(FT, P).T,
            g[ff + "Wscale_ug"].reshape(2 * FT, P).T, np.zeros((P, 6), np.float32),
            np.broadcast_to(g[ff + "Wscale_dp"][None, :], (P, D))], 1),
        "w_up": k_tiles(g[ff + "W_up"].T), "w_gate": k_tiles(g[ff + "W_gate"].T),
        "w_down": g[ff + "W_down"].T.reshape(FT, P, D).transpose(1, 0, 2).reshape(P, FT * D),
        "rows_a": np.concatenate([by_head(g[at + "q_w"]), by_head(g[at + "k_w"]), rank(g[at + "f_w2"]),
                                  per_channel(g[at + "q_conv_w"]), per_channel(g[at + "k_conv_w"]),
                                  per_channel(g[at + "dt_bias"]), a_log, fill(6)], 2).reshape(HEADS * P, A_COLS),
        "rows_b": np.concatenate([by_head(g[at + "v_w"]), rank(g[at + "g_w2"]), per_channel(g[at + "v_conv_w"]),
                                  per_channel(g[at + "g_b2"]), fill(11)], 2).reshape(HEADS * P, B_COLS),
        "o_w": g[at + "o_w"],
    }
    nc = bacc.Bacc("TRN2", target_bir_lowering=False, num_devices=1)
    feed, io = {}, {}
    for name, v in arrays.items():
        v = np.ascontiguousarray(v)
        feed["in_" + name] = v
        io[name] = nc.dram_tensor("in_" + name, v.shape, F32, kind="ExternalInput").ap()
    io["out"] = nc.dram_tensor("out", [TOK, D], F32, kind="ExternalOutput").ap()
    build(nc, io)
    r = run_bass_kernel_spmd(nc, [feed], core_ids=[0])
    return r.results[0]["out"].reshape(BATCH, SEQ, D)
```

```python
from contextlib import ExitStack

import numpy as np
import concourse.bass as bass
from concourse import mybir

F32 = mybir.dt.float32
U32 = mybir.dt.uint32
ALU = mybir.AluOpType
ACT = mybir.ActivationFunctionType
AX_X = mybir.AxisListType.X

P = 128
BATCH, SEQ, D = 2, 512, 256
HEADS = 16
TOK = BATCH * SEQ
NCH = TOK // P
CPB = SEQ // P
KT = D // P
INTER = 1024
FT = INTER // P
TAPS = 4
LEVELS = 7
LOW = 3
SUB = 1 << LOW
HIGH = LEVELS - LOW
C_MASK = 2 * P
C_SPREAD = C_MASK + 64 * LEVELS
C_BLOCK = C_SPREAD + SUB * P
C_STEP = C_BLOCK + P // SUB
CST_COLS = C_STEP + SUB
EPS_LN, EPS_L2, EPS_NORM = 1e-5, 1e-6, 1e-5

A_Q, A_K, A_F2, A_C = 0, KT * P, 2 * KT * P, 2 * KT * P + P
A_COLS = A_C + 16
B_V, B_G2, B_C = 0, KT * P, KT * P + P
B_COLS = B_C + 16
SUB_STEPS = 4 + 2 * (SUB - 1)
SC_PER_HEAD = LEVELS + 2
PJ_PREP, PJ_LEVEL, PJ_SCAN = 5, 3, 3


def wait(eng, sem, value):
    if isinstance(value, int) and value <= 0:
        return
    eng.wait_ge(sem, value)


def scaled_count(level):
    return 2 + 3 * level


def setup_block(nc, io, sb, ps, names, rows_loaded):
    sem = {n: names.enter_context(nc.semaphore("setup_" + n)) for n in (
        "x_loaded", "const_loaded", "ffn_const_loaded", "small_w_loaded", "up_loaded", "gate_loaded", "down_loaded",
        "stats", "moments", "var", "rstd", "xn", "xn_T", "xn_T_copied", "signed_x", "x_mixed", "x_had", "x_had_copied",
        "w_scaled", "shared", "shared_copied", "beta_exp", "beta_step", "w_mixed", "w_had", "w_down_ready", "wdp_scaled",
        "gate_up", "silu", "y_ready", "down", "acc_ready", "hw_ready")}
    acc, xnT, lv, kq = sb["acc"], sb["xnT"], sb["lv"], sb["kq"]
    wa, wb, wc = sb["wa"], sb["wb"], sb["wc"]
    cst, ffc, small = sb["cst"], sb["oT"], sb["o_raw"]
    hadamard, ident = cst[:, 0:P], cst[:, P:2 * P]
    xn = [sb["vn"][n] for n in range(2)]
    y = lv[:, 0:FT * TOK].rearrange("p (f t) -> p f t", f=FT)
    w_up = lv[:, FT * TOK:FT * TOK + 2048].rearrange("p (k f) -> p k f", k=KT)
    w_gate = lv[:, FT * TOK + 2048:FT * TOK + 4096].rearrange("p (k f) -> p k f", k=KT)
    x_had = lv[:, FT * TOK + 4096:FT * TOK + 6144].rearrange("p (k t) -> p k t", k=KT)
    signed = [sb["g_sig"][0], sb["g_sig"][1]]
    mixed = [sb["k_hat"][0], sb["k_hat"][1]]
    wd = [kq[0], kq[1]]
    silu_t = [sb["q"], sb["a"]]
    su_ug, su_dp, wsc, wdp = ffc[:, 0:2], ffc[:, 2:10], ffc[:, 10:26], ffc[:, 32:288]
    wsc16, wdp32 = ffc[:, 288:304], ffc[:, 304:560]
    f_w1 = small[:, 0:256].rearrange("p (k n) -> p k n", k=KT)
    g_w1 = small[:, 256:512].rearrange("p (k n) -> p k n", k=KT)
    b_w = small[:, 512:544].rearrange("p (k n) -> p k n", k=KT)
    beta_tmp = small[:, 544:672]
    beta_tmp2 = small[:, 672:800]
    stats = [sb["v"][:, 16 * c:16 * c + 6] for c in range(NCH)]
    moments = [sb["v"][:, 128 + 4 * c:128 + 4 * c + 2] for c in range(NCH)]
    var_eps, rstd_all = sb["v"][:, 192:192 + NCH], sb["v"][:, 208:208 + NCH]
    rstd = [rstd_all[:, c:c + 1] for c in range(NCH)]

    def xn_tile(c):
        return xn[c // 4][:, (c % 4) * D:(c % 4 + 1) * D]

    with nc.Block() as block:
        @block.sync
        def _(sp):
            for n in range(BATCH):
                sp.dma_start(acc[:, n * CPB:(n + 1) * CPB, :],
                             io["x"][n * SEQ:(n + 1) * SEQ, :].rearrange("(c p) d -> p c d", p=P))\
                  .then_inc(sem["x_loaded"], 16)
            sp.dma_start(cst[:, :], io["consts"]).then_inc(sem["const_loaded"], 16)
            sp.dma_start(sb["hw"][:, :], io["o_norm_w"]).then_inc(sem["const_loaded"], 16)
            sp.dma_start(small[:, 0:544], io["small_w"]).then_inc(sem["small_w_loaded"], 16)
            sp.dma_start(w_gate, io["w_gate"]).then_inc(sem["gate_loaded"], 16)
            sp.dma_start(w_up, io["w_up"]).then_inc(sem["up_loaded"], 16)
            for h in range(2):
                sp.dma_start(wa[h][:, :], io["rows_a"][h * P:(h + 1) * P, :]).then_inc(rows_loaded["a", h], 16)
            sp.dma_start(wb[0][:, :], io["rows_b"][0:P, :]).then_inc(rows_loaded["b", 0], 16)
            sp.dma_start(wc[0][:, :], io["o_w"][0:P, :]).then_inc(rows_loaded["c", 0], 16)

        @block.gpsimd
        def _(pool):
            pool.wait_ge(sem["var"], NCH)
            pool.tensor_tensor(rstd_all, var_eps, sb["powers"][:, 0:NCH], ALU.pow).then_inc(sem["rstd"], 1)

        @block.scalar
        def _(act):
            act.dma_start(ffc[:, 0:288], io["ffn_consts"]).then_inc(sem["ffn_const_loaded"], 16)
            act.dma_start(wd[0][:, :], io["w_down"]).then_inc(sem["down_loaded"], 16)
            for c in range(NCH):
                act.wait_ge(sem["xn_T"], c + 1)
                act.activation(xnT[:, :, c * P:(c + 1) * P],
                               ps[:, 512 * c:512 * c + 2 * P].rearrange("p (k t) -> p k t", k=KT),
                               ACT.Copy).then_inc(sem["xn_T_copied"], 1)
            for n, dst in enumerate((sb["f1T"], sb["g1T"])):
                act.wait_ge(sem["shared"], n + 1)
                act.activation(dst[:, :], ps[:, 1024 * n:1024 * n + 1024], ACT.Copy).then_inc(sem["shared_copied"], 1)
            act.wait_ge(sem["shared"], 3)
            act.activation(beta_tmp, ps[:, 2048:2176], ACT.Exp, scale=-1.0).then_inc(sem["beta_exp"], 1)
            for k in range(KT):
                act.wait_ge(sem["x_had"], k + 1)
                act.activation(x_had[:, k, :], ps[:, 1024 * k:1024 * (k + 1)], ACT.Copy).then_inc(sem["x_had_copied"], 1)
            act.wait_ge(sem["w_scaled"], 1)
            for f in range(FT):
                act.wait_ge(sem["gate_up"], f + 1)
                if f >= 2:
                    act.wait_ge(sem["y_ready"], f - 1)
                act.activation(silu_t[f % 2][:, :], ps[:, 2048 * (f % 2):2048 * (f % 2) + 1024], ACT.Silu,
                               scale=wsc16[:, FT + f:FT + f + 1]).then_inc(sem["silu"], 1)

        @block.vector
        def _(dve):
            for c in range(NCH):
                dve.wait_ge(sem["x_loaded"], 16 * BATCH)
                dve.bn_stats(stats[c], acc[:, c, :]).then_inc(sem["stats"], 1)
            for c in range(NCH):
                dve.wait_ge(sem["stats"], c + 1)
                dve.bn_aggr(moments[c], stats[c]).then_inc(sem["moments"], 1)
            for c in range(NCH):
                dve.wait_ge(sem["moments"], c + 1)
                dve.tensor_scalar(var_eps[:, c:c + 1], moments[c][:, 1:2], EPS_LN, None, ALU.add)\
                   .then_inc(sem["var"], 1)
            for c in range(NCH):
                dve.wait_ge(sem["rstd"], 1)
                dve.tensor_scalar(xn_tile(c), acc[:, c, :], moments[c][:, 0:1], rstd[c], ALU.subtract,
                                  ALU.mult).then_inc(sem["xn"], 1)
            dve.wait_ge(sem["ffn_const_loaded"], 16)
            dve.tensor_scalar(wsc16, wsc, float(D) ** -0.5, None, ALU.mult).then_inc(sem["w_scaled"], 1)
            dve.tensor_scalar(wdp32, wdp, float(INTER) ** -0.5, None, ALU.mult).then_inc(sem["wdp_scaled"], 1)
            dve.wait_ge(sem["const_loaded"], 32)
            dve.tensor_scalar(sb["hw"][:, :], sb["hw"][:, :], 0.5, None, ALU.mult).then_inc(sem["hw_ready"], 1)
            dve.wait_ge(sem["xn_T_copied"], NCH)
            for k in range(KT):
                dve.tensor_scalar(signed[k][:, :], xnT[:, k, :], su_ug[:, k:k + 1], None, ALU.mult)\
                   .then_inc(sem["signed_x"], 1)
            dve.wait_ge(sem["signed_x"], 2)
            for k, op in enumerate((ALU.add, ALU.subtract)):
                dve.tensor_tensor(mixed[k][:, :], signed[0][:, :], signed[1][:, :], op).then_inc(sem["x_mixed"], 1)
            dve.wait_ge(sem["down_loaded"], 16)
            for n in range(3):
                s = 256 << n
                a = wd[n % 2][:, :].rearrange("p (n two s) -> p n two s", two=2, s=s)
                b = wd[(n + 1) % 2][:, :].rearrange("p (n two s) -> p n two s", two=2, s=s)
                wait(dve, sem["w_mixed"], 2 * n)
                for half, op in enumerate((ALU.add, ALU.subtract)):
                    dve.tensor_tensor(b[:, :, half, :], a[:, :, 0, :], a[:, :, 1, :], op).then_inc(sem["w_mixed"], 1)
            dve.wait_ge(sem["beta_exp"], 1)
            dve.tensor_scalar(beta_tmp2, beta_tmp, 1.0, None, ALU.add).then_inc(sem["beta_step"], 1)
            dve.wait_ge(sem["beta_step"], 1)
            dve.reciprocal(beta_tmp, beta_tmp2).then_inc(sem["beta_step"], 1)
            dve.wait_ge(sem["beta_step"], 2)
            dve.tensor_copy(sb["beta"][:, :].rearrange("p (h c) -> p h c", c=NCH),
                            beta_tmp.rearrange("p (c h) -> p h c", h=HEADS)).then_inc(sem["beta_step"], 1)
            dve.wait_ge(sem["w_had"], 1)
            dve.wait_ge(sem["wdp_scaled"], 1)
            for f in range(FT):
                dve.scalar_tensor_tensor(wd[0][:, D * f:D * f + D], ps[:, 2048 + D * f:2048 + D * f + D],
                                         su_dp[:, f:f + 1], wdp32, ALU.mult, ALU.mult).then_inc(sem["w_down_ready"], 1)
            for f in range(FT):
                dve.wait_ge(sem["silu"], f + 1)
                dve.scalar_tensor_tensor(y[:, f, :], ps[:, 2048 * (f % 2) + 1024:2048 * (f % 2) + 2048],
                                         wsc16[:, f:f + 1], silu_t[f % 2][:, :], ALU.mult, ALU.mult)\
                   .then_inc(sem["y_ready"], 1)
            for g in range(NCH // 2):
                dve.wait_ge(sem["down"], g + 1)
                dve.tensor_tensor(acc[:, 2 * g:2 * g + 2, :], acc[:, 2 * g:2 * g + 2, :],
                                  ps[:, 512 * g:512 * g + 512].rearrange("p (c d) -> p c d", c=2), ALU.add)\
                   .then_inc(sem["acc_ready"], 1)
            dve.wait_ge(sem["acc_ready"], NCH // 2)
            dve.wait_ge(sem["beta_step"], 3)
            dve.wait_ge(sem["hw_ready"], 1)

        @block.tensor
        def _(pe):
            pe.wait_ge(sem["const_loaded"], 32)
            for c in range(NCH):
                pe.wait_ge(sem["xn"], c + 1)
                for k in range(KT):
                    last = pe.transpose(ps[:, 512 * c + P * k:512 * c + P * (k + 1)],
                                        xn_tile(c)[:, P * k:P * (k + 1)], ident)
                last.then_inc(sem["xn_T"], 1)
            pe.wait_ge(sem["xn_T_copied"], NCH)
            pe.wait_ge(sem["small_w_loaded"], 16)
            for n, w in enumerate((f_w1, g_w1)):
                for b in range(BATCH):
                    for k in range(KT):
                        last = pe.matmul(ps[:, 1024 * n + SEQ * b:1024 * n + SEQ * (b + 1)], w[:, k, :],
                                         xnT[:, k, SEQ * b:SEQ * (b + 1)], start=(k == 0), stop=(k == KT - 1))
                last.then_inc(sem["shared"], 1)
            for c in range(NCH):
                for k in range(KT):
                    last = pe.matmul(ps[:, 2048 + HEADS * c:2048 + HEADS * (c + 1)], xnT[:, k, c * P:(c + 1) * P],
                                     b_w[:, k, :], start=(k == 0), stop=(k == KT - 1))
            last.then_inc(sem["shared"], 1)
            for k in range(KT):
                pe.wait_ge(sem["x_mixed"], k + 1)
                pe.wait_ge(sem["shared_copied"], k + 1)
                for b in range(BATCH):
                    last = pe.matmul(ps[:, 1024 * k + SEQ * b:1024 * k + SEQ * (b + 1)], hadamard,
                                     mixed[k][:, SEQ * b:SEQ * (b + 1)], start=True, stop=True)
                last.then_inc(sem["x_had"], 1)
            pe.wait_ge(sem["w_mixed"], 6)
            pe.wait_ge(sem["beta_exp"], 1)
            for n in range(4):
                last = pe.matmul(ps[:, 2048 + 512 * n:2048 + 512 * (n + 1)], hadamard,
                                 wd[1][:, 512 * n:512 * (n + 1)], start=True, stop=True)
            last.then_inc(sem["w_had"], 1)
            pe.wait_ge(sem["x_had_copied"], KT)
            pe.wait_ge(sem["gate_loaded"], 16)
            pe.wait_ge(sem["up_loaded"], 16)
            for f in range(FT):
                if f == 1:
                    pe.wait_ge(sem["w_down_ready"], FT)
                if f >= 2:
                    pe.wait_ge(sem["y_ready"], f - 1)
                for n, w in enumerate((w_gate, w_up)):
                    at = 2048 * (f % 2) + 1024 * n
                    for b in range(BATCH):
                        for k in range(KT):
                            last = pe.matmul(ps[:, at + SEQ * b:at + SEQ * (b + 1)], w[:, k, P * f:P * (f + 1)],
                                             x_had[:, k, SEQ * b:SEQ * (b + 1)], start=(k == 0), stop=(k == KT - 1))
                last.then_inc(sem["gate_up"], 1)
            pe.wait_ge(sem["y_ready"], FT)
            for g in range(NCH // 2):
                for c in (2 * g, 2 * g + 1):
                    for f in range(FT):
                        last = pe.matmul(ps[:, D * c:D * (c + 1)], y[:, f, c * P:(c + 1) * P],
                                         wd[0][:, D * f:D * (f + 1)], start=(f == 0), stop=(f == FT - 1))
                last.then_inc(sem["down"], 1)


def heads_block(nc, io, sb, ps, names, rows_loaded):
    def new(*ns):
        for n in ns:
            sem[n] = names.enter_context(nc.semaphore(n))
    sem = {}
    for (rows, parity), loaded in rows_loaded.items():
        sem[f"{rows}_rows_loaded{parity}"] = loaded
    new("zeroed", "stored")
    new("q_proj", "k_proj", "v_proj", "gate_proj", "g_proj", "ssq_ready", "ssk_ready", "vT_ready", "oT_ready",
        "out_ready", "scores_ready", "spread_ready", "tt_ready", "x_ready", "r_prod", "p1_ready", "u_ready",
        "o_ready", "ds_ready")
    new("pj_free", "sc_free")
    new("q_tap0", "k_tap0", "v_tap0", "q_raw", "k_raw", "v_raw", "q_silu", "k_silu", "v_silu", "q_sq", "k_sq",
        "gate_tanh", "z_abs", "z_exp", "z_ln", "a_ready", "a_scale", "bc_ready", "tc_ready", "xb_ready", "ub_ready",
        "o_copied", "o_sq", "khat_ready")
    new("q_taps", "k_taps", "v_taps", "at_ready", "at_low_ready", "low_masks_begun", "aq_ready", "atc_ready",
        "sub_step", "r_updated", "rhs_ready", "s_ready", "ssq_step", "ssk_step", "rq_ready", "c_ready",
        "gate_ready", "z_relu", "z_w", "z_step", "vn_ready", "norm_step", "on_ready", "ot_gated", "acc_added")
    new("scaled", "r_spread", "rq_root", "nk_root", "norm_root")

    cst, beta, hw = sb["cst"], sb["beta"], sb["hw"]
    ident = cst[:, P:2 * P]
    masks = [cst[:, C_MASK + 64 * l:C_MASK + 64 * (l + 1)] for l in range(LEVELS)]
    block_mask, step_mask = cst[:, C_BLOCK:C_BLOCK + P // SUB], cst[:, C_STEP:C_STEP + SUB]
    xnT, f1T, g1T, acc = sb["xnT"], sb["f1T"], sb["g1T"], sb["acc"]
    k_s, kq, aq, r_t, k_hat, vn, g_sig = (sb[n] for n in ("k", "kq", "aq", "r_t", "k_hat", "vn", "g_sig"))
    q_s, a_s, v_s, o_raw, oT = (sb[n] for n in ("q", "a", "v", "o_raw", "oT"))
    r_c = sb["r_c"][:, :].rearrange("p (c i) -> p c i", c=NCH)
    sub_tmp = sb["sub_tmp"][:, :].rearrange("p (c i) -> p c i", c=NCH)
    atc = sb["atc"][:, :].rearrange("p (c i) -> p c i", c=NCH)
    d = sb["d"]
    state, rhs, u_s = sb["state"], sb["rhs"], sb["u"]
    wa, wb, wc = sb["wa"], sb["wb"], sb["wc"]
    tiny = sb["tiny"]
    nk = [tiny[:, 64 * n:64 * n + 8] for n in range(2)]
    rq = [tiny[:, 64 * n + 16:64 * n + 24] for n in range(2)]
    rqd = [tiny[:, 64 * n + 24:64 * n + 32] for n in range(2)]
    rq2 = [tiny[:, 64 * n + 32:64 * n + 40] for n in range(2)]
    totc = [tiny[:, 64 * n + 40:64 * n + 48] for n in range(2)]
    ci = [tiny[:, 64 * n + 48:64 * n + 56] for n in range(2)]
    ssq_e, ssk_e = tiny[:, 162:170], tiny[:, 170:178]
    inv_root, root = sb["powers"][:, 0:NCH], sb["powers"][:, NCH:2 * NCH]
    sso, ms, rr, rs = (tiny[:, 128 + 8 * n:136 + 8 * n] for n in range(4))
    a_scale, half_gb = tiny[:, 160:161], tiny[:, 161:162]
    def by_chunk(ap):
        return ap.rearrange("p (c i) -> p c i", c=NCH)

    lv = sb["lv"]
    at_b = {l: by_chunk(lv[:, TOK * n:TOK * (n + 1)]) for n, l in enumerate(range(LOW, LEVELS))}
    x_b = {l: by_chunk(lv[:, TOK * (HIGH + n):TOK * (HIGH + n + 1)]) for n, l in enumerate(range(LOW, LEVELS))}
    at_low = by_chunk(lv[:, 2 * HIGH * TOK:(2 * HIGH + 1) * TOK])
    raw = [lv[:, (2 * HIGH + 1 + n) * TOK:(2 * HIGH + 2 + n) * TOK] for n in range(2)]
    bc = lv[:, (2 * HIGH + 3) * TOK:(2 * HIGH + 3) * TOK + 512]
    bc_a = bc[:, 0:(SUB - 1) * NCH * (SUB + 1)].rearrange("p (m c i) -> p m c i", m=SUB - 1, c=NCH)
    bc_last = bc[:, (SUB - 1) * NCH * (SUB + 1):].rearrange("p (c one) -> p c one", one=1)
    scaled_a = lv[:, (2 * HIGH + 3) * TOK + 512:(2 * HIGH + 3) * TOK + 512 + (SUB - 1) * NCH * SUB]\
        .rearrange("p (m c i) -> p m c i", m=SUB - 1, c=NCH)
    tot = lv[:, (2 * HIGH + 4) * TOK:(2 * HIGH + 5) * TOK]
    t_c = lv[:, (2 * HIGH + 5) * TOK:(2 * HIGH + 5) * TOK + TOK // 2]

    pj, sc = ps[:, 0:1024], ps[:, 1024:2048]
    tt_p = [ps[:, 2048 + 512 * n:2560 + 512 * n] for n in range(2)]
    x_p = [ps[:, 2048 + 512 * n:2304 + 512 * n] for n in range(2)]
    ru_p = [ps[:, 2304 + 512 * n:2560 + 512 * n] for n in range(2)]
    spread_p = tt_p[0]
    seq_a, seq_b = ps[:, 3072:3328], ps[:, 3584:3840]

    def halves(ap, l, half):
        return ap.rearrange("p (n two s) -> p n two s", two=2, s=1 << l)[:, :, half, :]

    def chunk_halves(ap, l, half):
        return ap.rearrange("p c (n two s) -> p c n two s", two=2, s=1 << l)[:, :, :, half, :]

    def packed(ap, l):
        return ap.rearrange("p c (n s) -> p c n s", s=1 << l)

    def tot_at(l):
        if l == 0:
            return a_s[:, :]
        at = 1024 - (2048 >> l)
        return tot[:, at:at + (1024 >> l)]

    def each(ap):
        return ap.unsqueeze(2).broadcast_to([P, NCH, P])

    def pj_before(i, n):
        if isinstance(i, int):
            if i == -1:
                return n
            if i == 0:
                return PJ_PREP + n
            if i == HEADS:
                return pj_before(HEADS - 1, 0) + PJ_LEVEL + PJ_SCAN + n
        full = PJ_PREP + PJ_LEVEL + PJ_SCAN
        return (i - 1) * full + (2 * PJ_PREP + PJ_LEVEL + n)

    def is_int(i):
        return isinstance(i, int)

    def step(h, l, half):
        return 2 * (HIGH * h + l - LOW) + half + 1

    def iterations(eng, body):
        body(-1, (0, 0), None, None)
        body(0, (0, 1), (0, 0), None)
        body(1, (1, 0), (0, 1), (0, 0))
        body(2, (1, 1), (1, 0), (0, 1))
        with eng.Fori(1, HEADS // 2 - 1) as g:
            body(2 * g + 1, (g + 1, 0), (g, 1), (g, 0))
            body(2 * g + 2, (g + 1, 1), (g + 1, 0), (g, 1))
        body(HEADS - 1, None, (HEADS // 2 - 1, 1), (HEADS // 2 - 1, 0))
        body(HEADS, None, None, (HEADS // 2 - 1, 1))

    def num(head):
        return 2 * head[0] + head[1]

    with nc.Block() as block:
        @block.sync
        def _(sp):
            def loads(i, b, m, s):
                if is_int(i) and i <= 0:
                    return

                def known(value):
                    return value if isinstance(value, int) else sp.snap(value)

                def counts(h):
                    return bass.ds(known(h * P), P), known(h - 1), known(h + 1)
                ready_b = counts(num(b)) if b else None
                ready_m = counts(num(m)) if m else None
                if b:
                    at, used, _ = ready_b
                    wait(sp, sem["a_scale"], used)
                    wait(sp, sem["g_proj"], used)
                    wait(sp, sem["k_silu"], used)
                    wait(sp, sem["z_relu"], used)
                    sp.dma_start(wa[b[1]][:, :], io["rows_a"][at, :]).then_inc(sem[f"a_rows_loaded{b[1]}"], 16)
                if m:
                    at, used, after = ready_m
                    wait(sp, sem["gate_ready"], used)
                    wait(sp, sem["v_silu"], used)
                    sp.dma_start(wb[m[1]][:, :], io["rows_b"][at, :]).then_inc(sem[f"b_rows_loaded{m[1]}"], 16)
                    wait(sp, sem["v_proj"], after)
                    sp.dma_start(wc[m[1]][:, :], io["o_w"][at, :]).then_inc(sem[f"c_rows_loaded{m[1]}"], 16)

            iterations(sp, loads)
            for n in range(BATCH):
                sp.wait_ge(sem["acc_added"], 2 * HEADS - 1 + n)
                sp.dma_start(io["out"][n * SEQ:(n + 1) * SEQ, :].rearrange("(c p) d -> p c d", p=P),
                             acc[:, n * CPB:(n + 1) * CPB, :]).then_inc(sem["stored"], 16)
            sp.wait_ge(sem["stored"], 16 * BATCH)

        @block.gpsimd
        def _(pool):
            for l in range(LOW, LEVELS):
                pool.memset(at_b[l], 0.0).then_inc(sem["zeroed"], 1)
                pool.memset(x_b[l], 0.0).then_inc(sem["zeroed"], 1)
            pool.memset(at_low, 0.0).then_inc(sem["zeroed"], 1)

            def body(i, b, m, s):
                def query_root():
                    pool.wait_ge(sem["ssq_step"], num(b) + 1)
                    wait(pool, sem["rq_ready"], 2 * (num(b) - 1))
                    pool.tensor_tensor(rq[b[1]], ssq_e, inv_root, ALU.pow).then_inc(sem["rq_root"], 1)

                def key_root():
                    pool.wait_ge(sem["ssk_step"], 2 * num(b) + 1)
                    wait(pool, sem["vn_ready"], num(b) - 1)
                    pool.tensor_tensor(nk[b[1]], ssk_e, root, ALU.pow).then_inc(sem["nk_root"], 1)

                def output_root():
                    pool.wait_ge(sem["norm_step"], 4 * num(s) + 3)
                    pool.tensor_tensor(rr, ms, inv_root, ALU.pow).then_inc(sem["norm_root"], 1)

                def first_scales():
                    h, p = num(m), m[1]
                    kk, qq = kq[p][:, 0:TOK], kq[p][:, TOK:2 * TOK]
                    wait(pool, sem["o_ready"], 4 * (h - 1))
                    wait(pool, sem["p1_ready"], 3 * (h - 1))
                    wait(pool, sem["k_silu"], h + 1)
                    wait(pool, sem["q_silu"], h + 1)
                    wait(pool, sem["a_ready"], h + 1)
                    pool.tensor_tensor(kk, k_s[p][:, :], a_s[:, :], ALU.mult).then_inc(sem["scaled"], 1)
                    pool.tensor_tensor(qq, q_s[:, :], a_s[:, :], ALU.mult).then_inc(sem["scaled"], 1)

                def scale(l):
                    h, p = num(m), m[1]
                    before = tot_at(l - 1).rearrange("p (n two) -> p n two", two=2)
                    n = TOK >> l
                    pool.wait_ge(sem["scores_ready"], SC_PER_HEAD * h + l + 1)
                    if l == 1:
                        pool.wait_ge(sem["k_sq"], h + 1)
                    pool.wait_ge(sem["scaled"], 23 * h + scaled_count(l - 1))
                    both = kq[p][:, :].rearrange("p (w n two s) -> p w n two s", w=2, two=2, s=1 << (l - 1))[:, :, :, 1, :]
                    pool.tensor_tensor(both, both, before[:, :, 0].unsqueeze(1).unsqueeze(3)
                                       .broadcast_to([P, 2, n, 1 << (l - 1)]), ALU.mult).then_inc(sem["scaled"], 1)
                    first = halves(k_s[p][:, :], l - 1, 0)
                    pool.tensor_tensor(first, first, before[:, :, 1].unsqueeze(2)
                                       .broadcast_to([P, n, 1 << (l - 1)]), ALU.mult).then_inc(sem["scaled"], 1)
                    if l == LEVELS:
                        wait(pool, sem["s_ready"], 5 * (h - 1))
                    after = totc[p] if l == LEVELS else tot_at(l)
                    pool.tensor_tensor(after, before[:, :, 0], before[:, :, 1], ALU.mult).then_inc(sem["scaled"], 1)

                def spread_blocks():
                    h, p = num(m), m[1]
                    wait(pool, sem["u_ready"], 4 * (h - 1))
                    pool.wait_ge(sem["sub_step"], SUB_STEPS * (h + 1))
                    nb = P // SUB
                    pool.tensor_tensor(r_t[p][:, :].rearrange("p (c n i) -> p c n i", c=NCH, n=nb),
                                       r_c.unsqueeze(2).broadcast_to([P, NCH, nb, SUB]),
                                       block_mask.unsqueeze(1).unsqueeze(3).broadcast_to([P, NCH, nb, SUB]),
                                       ALU.mult).then_inc(sem["r_spread"], 1)

                if m:
                    first_scales()
                    for l in (1, 2, 3, 4, 5):
                        scale(l)
                    spread_blocks()
                if b:
                    query_root()
                if m:
                    scale(6)
                if b:
                    key_root()
                if m:
                    scale(7)
                if s:
                    output_root()

            iterations(pool, body)

        @block.tensor
        def _(pe):
            def body(i, b, m, s):
                use = [0]
                hb, hm, hs = (num(x) if x else None for x in (b, m, s))

                def take_pj():
                    wait(pe, sem["pj_free"], pj_before(i, use[0]))
                    use[0] += 1

                def project(w, src, kts, done):
                    take_pj()
                    for n in range(BATCH):
                        for k in range(kts):
                            last = pe.matmul(pj[:, SEQ * n:SEQ * (n + 1)], w[:, P * k:P * (k + 1)],
                                             src[:, k, SEQ * n:SEQ * (n + 1)] if kts > 1
                                             else src[:, SEQ * n:SEQ * (n + 1)],
                                             start=(k == 0), stop=(k == kts - 1))
                    last.then_inc(done, 1)

                def scores(l):
                    p = m[1]
                    if l < 0:
                        pe.wait_ge(sem["k_silu"], hm + 1)
                        pe.wait_ge(sem["q_silu"], hm + 1)
                    else:
                        pe.wait_ge(sem["scaled"], 23 * hm + scaled_count(l) - min(l, 1))
                    wait(pe, sem["sc_free"], SC_PER_HEAD * hm + l + 1)
                    for c in range(NCH):
                        if l < 0:
                            moving = q_s[:, c * P:(c + 1) * P]
                        else:
                            moving = kq[p][:, :].rearrange("p (w c i) -> p w c i", w=2, c=NCH)[:, :, c, :]\
                                .rearrange("p w (n two s) -> p w n two s", two=2, s=1 << l)[:, :, :, 1, :]
                        last = pe.matmul(sc[:, c * P:(c + 1) * P], k_s[p][:, c * P:(c + 1) * P], moving,
                                         start=True, stop=True)
                    last.then_inc(sem["scores_ready"], 1)

                def spread():
                    pe.wait_ge(sem["atc_ready"], hm + 1)
                    pe.wait_ge(sem["c_ready"], hm + 1)
                    wait(pe, sem["r_updated"], 2 * HIGH * hm)
                    wide = NCH * (SUB + 1)
                    for n in range(SUB):
                        rows = cst[:, C_SPREAD + P * n:C_SPREAD + P * (n + 1)]
                        if n < SUB - 1:
                            pe.matmul(spread_p[:, wide * n:wide * (n + 1)], rows, atc, start=True, stop=True)
                        else:
                            last = pe.matmul(spread_p[:, wide * n:wide * n + NCH], rows, atc[:, :, SUB],
                                             start=True, stop=True)
                    last.then_inc(sem["spread_ready"], 1)

                def turn_t(l):
                    for n in range(BATCH):
                        if l == LOW:
                            pe.wait_ge(sem["r_spread"], hm + 1)
                            pe.wait_ge(sem["bc_ready"], hm + 1)
                            wait(pe, sem["r_updated"], 2 * HIGH * hm)
                        else:
                            pe.wait_ge(sem["r_updated"], step(hm, l - 1, n))
                        for c in range(CPB):
                            cc = n * CPB + c
                            last = pe.transpose(tt_p[n][:, c * P:(c + 1) * P], r_t[m[1]][:, cc * P:(cc + 1) * P],
                                                ident)
                        last.then_inc(sem["tt_ready"], 1)

                def x_product(l):
                    pe.wait_ge(sem["at_ready"], HIGH * hm + l - LOW + 1)
                    for n in range(BATCH):
                        pe.wait_ge(sem["tc_ready"], step(hm, l, n))
                        for c in range(CPB):
                            cc = n * CPB + c
                            last = pe.matmul(x_p[n][:, 64 * c:64 * (c + 1)], at_b[l][:, cc, :],
                                             t_c[:, 64 * cc:64 * (cc + 1)], start=True, stop=True)
                        last.then_inc(sem["x_ready"], 1)

                def r_product(l):
                    for n in range(BATCH):
                        pe.wait_ge(sem["xb_ready"], step(hm, l, n))
                        for c in range(CPB):
                            cc = n * CPB + c
                            last = pe.matmul(ru_p[n][:, 64 * c:64 * (c + 1)], x_b[l][:, cc, :],
                                             halves(r_t[m[1]][:, cc * P:(cc + 1) * P], l, 1), start=True, stop=True)
                        last.then_inc(sem["r_prod"], 1)

                def scan_state(c):
                    p = s[1]
                    pe.wait_ge(sem["s_ready"], 5 * hs + 2 * c - 1)
                    for n in range(BATCH):
                        at = (n * CPB + c) * P
                        last = pe.matmul(seq_a[:, n * P:(n + 1) * P], kq[p][:, at:at + P],
                                         state[c % 2][:, n * P:(n + 1) * P], start=True, stop=True)
                    last.then_inc(sem["p1_ready"], 1)

                def scan_u(c):
                    p = s[1]
                    if c == 0:
                        pe.wait_ge(sem["vn_ready"], hs + 1)
                        pe.wait_ge(sem["r_updated"], 2 * HIGH * (hs + 1))
                    else:
                        pe.wait_ge(sem["rhs_ready"], 3 * hs + c)
                    wait(pe, sem["o_copied"], 4 * hs + c)
                    for n in range(BATCH):
                        cc = n * CPB + c
                        rows = vn[p][:, cc * P:(cc + 1) * P] if c == 0 else rhs[:, n * P:(n + 1) * P]
                        last = pe.matmul(seq_b[:, n * P:(n + 1) * P], r_t[p][:, cc * P:(cc + 1) * P], rows,
                                         start=True, stop=True)
                    last.then_inc(sem["u_ready"], 1)

                def scan_out(c):
                    p = s[1]
                    pe.wait_ge(sem["ub_ready"], 4 * hs + c + 1)
                    if c == 0:
                        pe.wait_ge(sem["khat_ready"], hs + 1)
                        pe.wait_ge(sem["aq_ready"], (LEVELS + 1) * (hs + 1))
                    if c < CPB - 1:
                        for n in range(BATCH):
                            cc = n * CPB + c
                            last = pe.matmul(seq_a[:, n * P:(n + 1) * P], k_hat[p][:, cc * P:(cc + 1) * P],
                                             u_s[:, n * P:(n + 1) * P], start=True, stop=True)
                        last.then_inc(sem["ds_ready"], 1)
                    for n in range(BATCH):
                        cc = n * CPB + c
                        last = pe.matmul(seq_b[:, n * P:(n + 1) * P], aq[p][:, cc * P:(cc + 1) * P],
                                         u_s[:, n * P:(n + 1) * P], start=True, stop=(c == 0))
                        if c > 0:
                            last = pe.matmul(seq_b[:, n * P:(n + 1) * P], kq[p][:, TOK + cc * P:TOK + (cc + 1) * P],
                                             state[c % 2][:, n * P:(n + 1) * P], start=False, stop=True)
                    last.then_inc(sem["o_ready"], 1)

                def sums_of_squares(squared, done):
                    take_pj()
                    pe.wait_ge(squared, hb + 1)
                    for c in range(NCH):
                        last = pe.matmul(pj[:, c:c + 1], d[3][:, c * P:(c + 1) * P], sb["ones"][:, 0:1],
                                         start=True, stop=True)
                    last.then_inc(done, 1)

                def turn(src, dst, done):
                    for c in range(NCH):
                        last = pe.transpose(dst[:, c * P:(c + 1) * P], src[:, c * P:(c + 1) * P], ident)
                    last.then_inc(done, 1)

                def turn_v():
                    take_pj()
                    pe.wait_ge(sem["v_silu"], hm + 1)
                    turn(v_s, pj, sem["vT_ready"])

                def turn_o():
                    take_pj()
                    pe.wait_ge(sem["on_ready"], hs + 1)
                    turn(o_raw, pj, sem["oT_ready"])

                def turn_keys():
                    pe.wait_ge(sem["scaled"], 23 * (hm + 1))
                    pe.wait_ge(sem["sc_free"], SC_PER_HEAD * hm + LEVELS + 1)
                    turn(k_s[m[1]], sc, sem["scores_ready"])

                def out_product(half):
                    p = s[1]
                    take_pj()
                    if half == 0:
                        pe.wait_ge(sem["ot_gated"], hs + 1)
                        pe.wait_ge(sem[f"c_rows_loaded{p}"], 16 * (s[0] + 1))
                    for c in range(4):
                        cc = 4 * half + c
                        last = pe.matmul(pj[:, D * c:D * (c + 1)], oT[:, cc * P:(cc + 1) * P], wc[p][:, :],
                                         start=True, stop=True)
                    last.then_inc(sem["out_ready"], 1)

                if is_int(i) and i == -1:
                    pe.wait_ge(sem["a_rows_loaded0"], 16)
                    project(wa[0][:, A_F2:], f1T, 1, sem["g_proj"])
                    project(wa[0][:, A_Q:], xnT, KT, sem["q_proj"])
                    project(wa[0][:, A_K:], xnT, KT, sem["k_proj"])
                    sums_of_squares(sem["q_sq"], sem["ssq_ready"])
                    sums_of_squares(sem["k_sq"], sem["ssk_ready"])
                    return

                if m:
                    scores(-1)
                if s:
                    scan_u(0)
                if b:
                    pe.wait_ge(sem[f"a_rows_loaded{b[1]}"], 16 * (b[0] + 1))
                    project(wa[b[1]][:, A_Q:], xnT, KT, sem["q_proj"])
                if m:
                    scores(0)
                if s:
                    scan_out(0)
                if b:
                    project(wa[b[1]][:, A_K:], xnT, KT, sem["k_proj"])
                if m:
                    scores(1)
                if s:
                    scan_state(1)
                if m:
                    pe.wait_ge(sem[f"b_rows_loaded{m[1]}"], 16 * (m[0] + 1))
                    project(wb[m[1]][:, B_V:], xnT, KT, sem["v_proj"])
                    scores(2)
                if s:
                    scan_u(1)
                if m:
                    project(wb[m[1]][:, B_G2:], g1T, 1, sem["gate_proj"])
                    scores(3)
                    spread()
                if s:
                    scan_out(1)
                if b:
                    sums_of_squares(sem["q_sq"], sem["ssq_ready"])
                if m:
                    scores(4)
                if s:
                    scan_state(2)
                if b:
                    sums_of_squares(sem["k_sq"], sem["ssk_ready"])
                if s:
                    scan_u(2)
                if m:
                    scores(5)
                if b:
                    project(wa[b[1]][:, A_F2:], f1T, 1, sem["g_proj"])
                if s:
                    scan_out(2)
                if m:
                    turn_t(3)
                    scores(6)
                if s:
                    scan_state(3)
                if m:
                    x_product(3)
                if s:
                    scan_u(3)
                if m:
                    r_product(3)
                if s:
                    scan_out(3)
                if m:
                    turn_t(4)
                    turn_v()
                    x_product(4)
                    r_product(4)
                    turn_keys()
                    turn_t(5)
                    x_product(5)
                if s:
                    turn_o()
                if m:
                    r_product(5)
                if m:
                    turn_t(6)
                if s:
                    out_product(0)
                if m:
                    x_product(6)
                if s:
                    out_product(1)
                if m:
                    r_product(6)

            iterations(pe, body)

        @block.scalar
        def _(act):
            def body(i, b, m, s):
                hb, hm, hs = (num(x) if x else None for x in (b, m, s))

                def out_of_pj(name, dst, w, buf, h):
                    act.wait_ge(sem[name + "_proj"], h + 1)
                    act.activation(dst[:, :], pj, ACT.Copy, scale=w).then_inc(sem[name + "_tap0"], 1)
                    act.activation(buf, pj, ACT.Copy).then_inc(sem[name + "_raw"], 1)
                    act.wait_ge(sem[name + "_raw"], h + 1)
                    act.sem_inc(sem["pj_free"], 1)

                def q_out():
                    wait(act, sem["scaled"], 23 * (hb - 1) + 2)
                    wait(act, sem["scores_ready"], SC_PER_HEAD * (hb - 1) + 1)
                    wait(act, sem["q_sq"], hb)
                    wait(act, sem["v_taps"], 3 * (hb - 1))
                    act.wait_ge(sem[f"a_rows_loaded{b[1]}"], 16 * (b[0] + 1))
                    out_of_pj("q", q_s, wa[b[1]][:, A_C + 3:A_C + 4], raw[0], hb)

                def k_out():
                    wait(act, sem["scores_ready"], SC_PER_HEAD * (hb - 1))
                    wait(act, sem["k_taps"], 3 * hb)
                    out_of_pj("k", k_s[b[1]], wa[b[1]][:, A_C + 7:A_C + 8], raw[1], hb)

                def v_out():
                    wait(act, sem["vT_ready"], hm)
                    act.wait_ge(sem[f"b_rows_loaded{m[1]}"], 16 * (m[0] + 1))
                    wait(act, sem["q_taps"], 3 * (hm + 2) if b else 3 * (hm + 1))
                    out_of_pj("v", v_s, wb[m[1]][:, B_C + 3:B_C + 4], raw[0], hm)

                def silu(name, buf, h):
                    act.wait_ge(sem[name + "_taps"], 3 * (h + 1))
                    act.activation(buf[:, :], buf[:, :], ACT.Silu).then_inc(sem[name + "_silu"], 1)

                def square(src, done, silued, free):
                    act.wait_ge(silued, hb + 1)
                    wait(act, *free)
                    act.activation(d[3][:, :], src[:, :], ACT.Square).then_inc(done, 1)

                def gate():
                    act.wait_ge(sem["gate_proj"], hm + 1)
                    act.activation(half_gb, wb[m[1]][:, B_C + 4:B_C + 5], ACT.Copy, scale=0.5)\
                       .then_inc(sem["gate_tanh"], 1)
                    act.wait_ge(sem["gate_tanh"], 2 * hm + 1)
                    wait(act, sem["ot_gated"], hm - 1)
                    act.activation(g_sig[m[1]][:, :], pj, ACT.Tanh, bias=half_gb, scale=0.5)\
                       .then_inc(sem["gate_tanh"], 1)
                    act.wait_ge(sem["gate_tanh"], 2 * hm + 2)
                    act.sem_inc(sem["pj_free"], 1)

                def decay_abs():
                    act.wait_ge(sem["g_proj"], hb + 1)
                    wait(act, sem["z_step"], 3 * hb)
                    act.activation(d[0][:, :], pj, ACT.Abs, bias=wa[b[1]][:, A_C + 8:A_C + 9])\
                       .then_inc(sem["z_abs"], 1)

                def decay_exp():
                    wait(act, sem["a_ready"], hb)
                    act.activation(a_scale, wa[b[1]][:, A_C + 9:A_C + 10], ACT.Exp).then_inc(sem["a_scale"], 1)
                    act.wait_ge(sem["z_abs"], hb + 1)
                    act.activation(d[1][:, :], d[0][:, :], ACT.Exp, scale=-1.0).then_inc(sem["z_exp"], 1)

                def decay_ln():
                    act.wait_ge(sem["z_w"], hb + 1)
                    if not (is_int(i) and i == -1):
                        act.wait_ge(sem["ssk_ready"], hb + 1)
                    act.activation(d[3][:, :], d[0][:, :], ACT.Ln).then_inc(sem["z_ln"], 1)

                def decay_out():
                    act.wait_ge(sem["z_step"], 3 * hb + 3)
                    wait(act, sem["scaled"], 23 * (hb - 1) + scaled_count(1))
                    act.wait_ge(sem["a_scale"], hb + 1)
                    act.activation(a_s[:, :], d[1][:, :], ACT.Exp, scale=a_scale).then_inc(sem["a_ready"], 1)

                def u_out(c):
                    act.wait_ge(sem["u_ready"], 4 * hs + c + 1)
                    wait(act, sem["o_ready"], 4 * hs + c)
                    wait(act, sem["ds_ready"], 3 * hs + min(c, CPB - 1))
                    act.activation(u_s[:, :], seq_b, ACT.Copy).then_inc(sem["ub_ready"], 1)

                def o_out(c):
                    act.wait_ge(sem["o_ready"], 4 * hs + c + 1)
                    if c == 0:
                        wait(act, sem["oT_ready"], hs)
                    act.activation(o_raw[:, :].rearrange("p (b c v) -> p b c v", b=BATCH, c=CPB)[:, :, c, :],
                                   seq_b.rearrange("p (b v) -> p b v", b=BATCH), ACT.Copy)\
                       .then_inc(sem["o_copied"], 1)

                def o_square():
                    act.wait_ge(sem["o_copied"], 4 * hs + 4)
                    wait(act, sem["out_ready"], 2 * hs)
                    act.activation(oT[:, :], o_raw[:, :], ACT.Square).then_inc(sem["o_sq"], 1)

                def spread_out():
                    act.wait_ge(sem["spread_ready"], hm + 1)
                    wait(act, sem["sub_step"], SUB_STEPS * hm)
                    act.activation(bc, spread_p, ACT.Copy).then_inc(sem["bc_ready"], 1)

                def t_out(l):
                    for n in range(BATCH):
                        act.wait_ge(sem["tt_ready"], step(hm, l, n))
                        wait(act, sem["x_ready"], step(hm, l - 1, n))
                        act.activation(packed(by_chunk(t_c)[:, n * CPB:(n + 1) * CPB, :], l),
                                       chunk_halves(tt_p[n].rearrange("p (c i) -> p c i", c=CPB), l, 0), ACT.Copy)\
                           .then_inc(sem["tc_ready"], 1)

                def x_out(l):
                    for n in range(BATCH):
                        act.wait_ge(sem["x_ready"], step(hm, l, n))
                        if isinstance(hm, int) and hm == 0 and l == LOW:
                            act.wait_ge(sem["zeroed"], 2 * HIGH + 1)
                        wait(act, sem["r_prod"], step(hm - 1, l, n))
                        act.activation(chunk_halves(x_b[l][:, n * CPB:(n + 1) * CPB, :], l, 0),
                                       packed(x_p[n].rearrange("p (c i) -> p c i", c=CPB), l), ACT.Copy)\
                           .then_inc(sem["xb_ready"], 1)

                def keys_out():
                    act.wait_ge(sem["scores_ready"], SC_PER_HEAD * (hm + 1))
                    wait(act, sem["ds_ready"], 3 * (hm - 1))
                    act.activation(k_hat[m[1]][:, :], sc, ACT.Copy).then_inc(sem["khat_ready"], 1)
                    act.wait_ge(sem["khat_ready"], hm + 1)
                    act.sem_inc(sem["sc_free"], 1)

                if is_int(i) and i == -1:
                    decay_abs()
                    decay_exp()
                    q_out()
                    decay_ln()
                    k_out()
                    decay_out()
                    silu("q", q_s, hb)
                    square(q_s, sem["q_sq"], sem["q_silu"], (sem["z_step"], 3))
                    silu("k", k_s[0], hb)
                    square(k_s[0], sem["k_sq"], sem["k_silu"], (sem["ssq_ready"], 1))
                    return

                if s:
                    u_out(0)
                if b:
                    q_out()
                if s:
                    o_out(0)
                if b:
                    k_out()
                    silu("q", q_s, hb)
                    square(q_s, sem["q_sq"], sem["q_silu"], (sem["z_step"], 3 * hb))
                if m:
                    v_out()
                if s:
                    u_out(1)
                if b:
                    silu("k", k_s[b[1]], hb)
                if m:
                    gate()
                    spread_out()
                if s:
                    o_out(1)
                if b:
                    square(k_s[b[1]], sem["k_sq"], sem["k_silu"], (sem["ssq_ready"], hb + 1))
                if s:
                    u_out(2)
                if m:
                    silu("v", v_s, hm)
                if b:
                    decay_abs()
                if s:
                    o_out(2)
                if m:
                    t_out(3)
                    x_out(3)
                if s:
                    u_out(3)
                if b:
                    decay_exp()
                if s:
                    o_out(3)
                if m:
                    t_out(4)
                if s:
                    o_square()
                if m:
                    x_out(4)
                    t_out(5)
                if b:
                    decay_ln()
                if m:
                    x_out(5)
                    keys_out()
                    t_out(6)
                if b:
                    decay_out()
                if m:
                    x_out(6)

            iterations(act, body)

        @block.vector
        def _(dve):
            def body(i, b, m, s):
                hb, hm, hs = (num(x) if x else None for x in (b, m, s))

                def conv(name, dst, src, w, at, h, ns):
                    for n in ns:
                        if n == 1:
                            dve.wait_ge(sem[name + "_tap0"], h + 1)
                            dve.wait_ge(sem[name + "_raw"], h + 1)
                        else:
                            dve.wait_ge(sem[name + "_taps"], 3 * h + n - 1)
                        y = dst[:, :].rearrange("p (b t) -> p b t", b=BATCH)[:, :, n:]
                        x = src.rearrange("p (b t) -> p b t", b=BATCH)[:, :, 0:SEQ - n]
                        dve.scalar_tensor_tensor(y, x, w[:, at + TAPS - 1 - n:at + TAPS - n], y, ALU.mult, ALU.add)\
                           .then_inc(sem[name + "_taps"], 1)

                def query_factors():
                    p = m[1]
                    dve.wait_ge(sem["rq_root"], hm + 1)
                    wait(dve, sem["norm_step"], 4 * (hm - 1))
                    dve.tensor_scalar(rqd[p], rq[p], float(P) ** -0.5, None, ALU.mult).then_inc(sem["rq_ready"], 1)
                    dve.wait_ge(sem["rq_ready"], 2 * hm + 1)
                    dve.scalar_tensor_tensor(rq2[p], rqd[p], 1.0 / P, rqd[p], ALU.mult, ALU.mult)\
                       .then_inc(sem["rq_ready"], 1)

                def diagonal():
                    dve.wait_ge(sem["scores_ready"], SC_PER_HEAD * hm + 1)
                    wait(dve, sem["o_ready"], 4 * (hm - 1))
                    dve.tensor_tensor(by_chunk(aq[m[1]][:, :]), by_chunk(sc),
                                      ident.unsqueeze(1).broadcast_to([P, NCH, P]), ALU.mult)\
                       .then_inc(sem["aq_ready"], 1)
                    dve.wait_ge(sem["aq_ready"], (LEVELS + 1) * hm + 1)
                    dve.sem_inc(sem["sc_free"], 1)

                def level_masks(l):
                    p = m[1]
                    mask = masks[l].unsqueeze(1).broadcast_to([P, NCH, 64])
                    keys, queries = by_chunk(sc)[:, :, 0:64], by_chunk(sc)[:, :, 64:128]
                    dve.wait_ge(sem["scores_ready"], SC_PER_HEAD * hm + l + 2)
                    if isinstance(hm, int) and hm == 0 and l == 0:
                        dve.wait_ge(sem["zeroed"], 2 * HIGH + 1)
                    dve.wait_ge(sem["aq_ready"], (LEVELS + 1) * hm + l + 1)
                    if l < LOW:
                        wait(dve, sem["atc_ready"], hm)
                        dve.sem_inc(sem["low_masks_begun"], 1)
                        dve.copy_predicated(chunk_halves(at_low, l, 1), packed(mask.bitcast(U32), l),
                                            packed(keys, l)).then_inc(sem["at_low_ready"], 1)
                    else:
                        wait(dve, sem["x_ready"], step(hm - 1, l, 1))
                        dve.tensor_tensor(chunk_halves(at_b[l], l, 1), packed(keys, l), packed(mask, l), ALU.mult)\
                           .then_inc(sem["at_ready"], 1)
                    dve.copy_predicated(chunk_halves(by_chunk(aq[p][:, :]), l, 1), packed(mask.bitcast(U32), l),
                                        packed(queries, l)).then_inc(sem["aq_ready"], 1)
                    if l < LOW:
                        dve.wait_ge(sem["at_low_ready"], LOW * hm + l + 1)
                    else:
                        dve.wait_ge(sem["at_ready"], HIGH * hm + l - LOW + 1)
                    dve.wait_ge(sem["aq_ready"], (LEVELS + 1) * hm + l + 2)
                    dve.sem_inc(sem["sc_free"], 1)

                def gather_low():
                    dve.wait_ge(sem["at_low_ready"], LOW * (hm + 1))
                    wait(dve, sem["spread_ready"], hm)
                    dve.tensor_reduce(atc[:, :, 0:SUB], at_low.rearrange("p c (n i) -> p c i n", i=SUB), AX_X,
                                      ALU.add).then_inc(sem["atc_ready"], 1)

                def substitute(ns):
                    if ns[0] == 0:
                        dve.wait_ge(sem["bc_ready"], hm + 1)
                        wait(dve, sem["r_spread"], hm)
                        c_low = bc_a[:, :, :, SUB].rearrange("p m c -> p c m")
                        dve.tensor_tensor(scaled_a[:, :, :, 0:SUB - 1], bc_a[:, :, :, 0:SUB - 1],
                                          c_low.unsqueeze(1).broadcast_to([P, SUB - 1, NCH, SUB - 1]), ALU.mult)\
                           .then_inc(sem["sub_step"], 1)
                        dve.tensor_tensor(scaled_a[:, :, :, SUB - 1], bc_a[:, :, :, SUB - 1],
                                          bc_last.rearrange("p c one -> p one c").broadcast_to([P, SUB - 1, NCH]),
                                          ALU.mult).then_inc(sem["sub_step"], 1)
                        dve.tensor_tensor(r_c[:, :, 0:SUB - 1], c_low,
                                          step_mask[:, 0:SUB - 1].unsqueeze(1).broadcast_to([P, NCH, SUB - 1]),
                                          ALU.mult).then_inc(sem["sub_step"], 1)
                        dve.tensor_tensor(r_c[:, :, SUB - 1:SUB], bc_last,
                                          step_mask[:, SUB - 1:SUB].unsqueeze(1).broadcast_to([P, NCH, 1]),
                                          ALU.mult).then_inc(sem["sub_step"], 1)
                    for n in ns:
                        left = SUB - 1 - n
                        dve.wait_ge(sem["sub_step"], SUB_STEPS * hm + 4 + 2 * n)
                        dve.tensor_tensor(sub_tmp[:, :, n + 1:], scaled_a[:, n, :, n + 1:],
                                          r_c[:, :, n:n + 1].broadcast_to([P, NCH, left]), ALU.mult)\
                           .then_inc(sem["sub_step"], 1)
                        dve.wait_ge(sem["sub_step"], SUB_STEPS * hm + 5 + 2 * n)
                        dve.tensor_tensor(r_c[:, :, n + 1:], r_c[:, :, n + 1:], sub_tmp[:, :, n + 1:], ALU.subtract)\
                           .then_inc(sem["sub_step"], 1)

                def update_r(l):
                    for n in range(BATCH):
                        dve.wait_ge(sem["r_prod"], step(hm, l, n))
                        r = chunk_halves(by_chunk(r_t[m[1]][:, :])[:, n * CPB:(n + 1) * CPB, :], l, 1)
                        dve.tensor_tensor(r, r, packed(ru_p[n].rearrange("p (c i) -> p c i", c=CPB), l),
                                          ALU.subtract).then_inc(sem["r_updated"], 1)

                def right_side(c):
                    dve.wait_ge(sem["p1_ready"], 3 * hs + c)
                    wait(dve, sem["u_ready"], 4 * hs + c)
                    dve.tensor_tensor(rhs[:, :].rearrange("p (b v) -> p b v", b=BATCH),
                                      vn[s[1]][:, :].rearrange("p (b c v) -> p b c v", b=BATCH, c=CPB)[:, :, c, :],
                                      seq_a.rearrange("p (b v) -> p b v", b=BATCH), ALU.subtract)\
                       .then_inc(sem["rhs_ready"], 1)

                def next_state(c):
                    dve.wait_ge(sem["ds_ready"], 3 * hs + c + 1)
                    wait(dve, sem["o_ready"], 4 * hs + c)
                    nxt = state[(c + 1) % 2]
                    if c == 0:
                        dve.tensor_copy(nxt[:, :], seq_a).then_inc(sem["s_ready"], 1)
                    else:
                        for n in range(BATCH):
                            cc = n * CPB + c
                            dve.scalar_tensor_tensor(nxt[:, n * P:(n + 1) * P], state[c % 2][:, n * P:(n + 1) * P],
                                                     totc[s[1]][:, cc:cc + 1], seq_a[:, n * P:(n + 1) * P],
                                                     ALU.mult, ALU.add).then_inc(sem["s_ready"], 1)

                def query_sums():
                    dve.wait_ge(sem["ssq_ready"], hb + 1)
                    wait(dve, sem["rq_root"], hb)
                    dve.tensor_scalar(ssq_e, pj[:, 0:NCH], EPS_L2, None, ALU.add).then_inc(sem["ssq_step"], 1)
                    dve.wait_ge(sem["ssq_step"], hb + 1)
                    dve.sem_inc(sem["pj_free"], 1)

                def key_sums():
                    dve.wait_ge(sem["ssk_ready"], hb + 1)
                    wait(dve, sem["nk_root"], hb)
                    dve.tensor_scalar(ssk_e, pj[:, 0:NCH], EPS_L2, None, ALU.add).then_inc(sem["ssk_step"], 1)
                    dve.wait_ge(sem["ssk_step"], 2 * hb + 1)
                    dve.sem_inc(sem["pj_free"], 1)
                    dve.reciprocal(ci[b[1]], ssk_e).then_inc(sem["ssk_step"], 1)
                    dve.wait_ge(sem["ssk_step"], 2 * hb + 2)
                    wait(dve, sem["spread_ready"], hb)
                    dve.tensor_tensor(atc[:, :, SUB], ci[b[1]], beta[:, bass.ds(hb * NCH, NCH)], ALU.mult)\
                       .then_inc(sem["c_ready"], 1)

                def gate():
                    dve.wait_ge(sem["gate_tanh"], 2 * hm + 2)
                    dve.tensor_scalar(g_sig[m[1]][:, :], g_sig[m[1]][:, :], hw[:, 0:1], hw[:, 0:1], ALU.mult,
                                      ALU.add).then_inc(sem["gate_ready"], 1)

                def relu_of_z():
                    dve.wait_ge(sem["z_abs"], hb + 1)
                    dve.tensor_scalar(d[2][:, :], pj, wa[b[1]][:, A_C + 8:A_C + 9], 0.0, ALU.add, ALU.max)\
                       .then_inc(sem["z_relu"], 1)
                    dve.wait_ge(sem["z_relu"], hb + 1)
                    dve.sem_inc(sem["pj_free"], 1)

                def one_plus_x():
                    dve.wait_ge(sem["z_exp"], hb + 1)
                    dve.tensor_scalar(d[0][:, :], d[1][:, :], 1.0, None, ALU.add).then_inc(sem["z_w"], 1)
                    dve.wait_ge(sem["z_w"], hb + 1)
                    dve.scalar_tensor_tensor(d[1][:, :], d[0][:, :], 1.0, d[1][:, :], ALU.subtract, ALU.subtract)\
                       .then_inc(sem["z_step"], 1)

                def minus_softplus():
                    dve.wait_ge(sem["z_ln"], hb + 1)
                    dve.wait_ge(sem["z_step"], 3 * hb + 1)
                    dve.tensor_tensor(d[1][:, :], d[1][:, :], d[3][:, :], ALU.subtract).then_inc(sem["z_step"], 1)
                    dve.wait_ge(sem["z_step"], 3 * hb + 2)
                    dve.tensor_tensor(d[1][:, :], d[1][:, :], d[2][:, :], ALU.subtract).then_inc(sem["z_step"], 1)

                def scaled_v():
                    dve.wait_ge(sem["vT_ready"], hm + 1)
                    dve.wait_ge(sem["nk_root"], hm + 1)
                    wait(dve, sem["rhs_ready"], 3 * (hm - 1))
                    wait(dve, sem["u_ready"], 4 * (hm - 1))
                    dve.tensor_tensor(by_chunk(vn[m[1]][:, :]), by_chunk(pj), each(nk[m[1]]), ALU.mult)\
                       .then_inc(sem["vn_ready"], 1)
                    dve.wait_ge(sem["vn_ready"], hm + 1)
                    dve.sem_inc(sem["pj_free"], 1)

                def norm_sums():
                    dve.wait_ge(sem["o_sq"], hs + 1)
                    dve.tensor_reduce(sso, by_chunk(oT[:, :]), AX_X, ALU.add).then_inc(sem["norm_step"], 1)
                    dve.wait_ge(sem["norm_step"], 4 * hs + 1)
                    dve.wait_ge(sem["rq_ready"], 2 * hs + 2)
                    wait(dve, sem["norm_root"], hs)
                    dve.tensor_tensor(ms, sso, rq2[s[1]], ALU.mult).then_inc(sem["norm_step"], 1)
                    dve.wait_ge(sem["norm_step"], 4 * hs + 2)
                    dve.tensor_scalar(ms, ms, EPS_NORM, None, ALU.add).then_inc(sem["norm_step"], 1)

                def normalize():
                    dve.wait_ge(sem["norm_root"], hs + 1)
                    dve.tensor_tensor(rs, rr, rqd[s[1]], ALU.mult).then_inc(sem["norm_step"], 1)
                    dve.wait_ge(sem["norm_step"], 4 * hs + 4)
                    dve.tensor_tensor(by_chunk(o_raw[:, :]), by_chunk(o_raw[:, :]), each(rs), ALU.mult)\
                       .then_inc(sem["on_ready"], 1)

                def gated():
                    dve.wait_ge(sem["oT_ready"], hs + 1)
                    dve.wait_ge(sem["gate_ready"], hs + 1)
                    dve.tensor_tensor(oT[:, :], pj, g_sig[s[1]][:, :], ALU.mult).then_inc(sem["ot_gated"], 1)
                    dve.wait_ge(sem["ot_gated"], hs + 1)
                    dve.sem_inc(sem["pj_free"], 1)

                def add_out(half):
                    dve.wait_ge(sem["out_ready"], 2 * hs + half + 1)
                    part = acc[:, 4 * half:4 * half + 4, :]
                    dve.tensor_tensor(part, part, pj.rearrange("p (c d) -> p c d", c=4), ALU.add)\
                       .then_inc(sem["acc_added"], 1)
                    dve.wait_ge(sem["acc_added"], 2 * hs + half + 1)
                    dve.sem_inc(sem["pj_free"], 1)

                if is_int(i) and i == -1:
                    relu_of_z()
                    one_plus_x()
                    conv("q", q_s, raw[0], wa[0], A_C, hb, (1, 2, 3))
                    minus_softplus()
                    conv("k", k_s[0], raw[1], wa[0], A_C + 4, hb, (1, 2, 3))
                    query_sums()
                    key_sums()
                    return

                if m:
                    query_factors()
                    diagonal()
                    level_masks(0)
                if b:
                    conv("q", q_s, raw[0], wa[b[1]], A_C, hb, (1, 2))
                if s:
                    next_state(0)
                if b:
                    conv("q", q_s, raw[0], wa[b[1]], A_C, hb, (3,))
                if m:
                    level_masks(1)
                if b:
                    conv("k", k_s[b[1]], raw[1], wa[b[1]], A_C + 4, hb, (1,))
                if s:
                    right_side(1)
                if b:
                    conv("k", k_s[b[1]], raw[1], wa[b[1]], A_C + 4, hb, (2,))
                if m:
                    level_masks(2)
                    gather_low()
                if b:
                    conv("k", k_s[b[1]], raw[1], wa[b[1]], A_C + 4, hb, (3,))
                if m:
                    level_masks(3)
                    conv("v", v_s, raw[0], wb[m[1]], B_C, hm, (1,))
                    substitute((0, 1))
                if s:
                    next_state(1)
                if m:
                    substitute((2, 3))
                if b:
                    query_sums()
                if m:
                    substitute((4, 5, 6))
                    level_masks(4)
                if s:
                    right_side(2)
                if b:
                    key_sums()
                if m:
                    conv("v", v_s, raw[0], wb[m[1]], B_C, hm, (2, 3))
                    gate()
                    level_masks(5)
                if b:
                    relu_of_z()
                if s:
                    next_state(2)
                if m:
                    level_masks(6)
                if s:
                    right_side(3)
                if m:
                    update_r(3)
                    scaled_v()
                if s:
                    norm_sums()
                if m:
                    update_r(4)
                if b:
                    one_plus_x()
                if s:
                    normalize()
                    gated()
                if m:
                    update_r(5)
                if b:
                    minus_softplus()
                if s:
                    add_out(0)
                    add_out(1)
                if m:
                    update_r(6)

            iterations(dve, body)


def build(nc, io):
    with ExitStack() as ctx:
        def buf(name, cols):
            return ctx.enter_context(nc.sbuf_tensor(name, [P, cols], F32))

        def pair(name, cols):
            return [buf(f"{name}{n}", cols) for n in range(2)]

        sb = {
            "xnT": ctx.enter_context(nc.sbuf_tensor("xnT", [P, KT, TOK], F32)),
            "acc": ctx.enter_context(nc.sbuf_tensor("acc", [P, NCH, D], F32)),
            "f1T": buf("f1T", TOK), "g1T": buf("g1T", TOK),
            "lv": buf("level_matrices", 14 * TOK),
            "k": pair("k", TOK), "kq": pair("kq", 2 * TOK), "aq": pair("aq", TOK), "r_t": pair("r_t", TOK),
            "k_hat": pair("k_hat", TOK), "vn": pair("vn", TOK), "g_sig": pair("g_sig", TOK),
            "q": buf("q", TOK), "a": buf("a", TOK), "v": buf("v", TOK),
            "r_c": buf("r_c", NCH * SUB), "sub_tmp": buf("sub_tmp", NCH * SUB), "atc": buf("atc", NCH * (SUB + 1)),
            "o_raw": buf("o_raw", TOK), "oT": buf("oT", TOK),
            "d": [buf(f"d{n}", TOK) for n in range(4)],
            "state": pair("state", BATCH * P), "rhs": buf("rhs", BATCH * P), "u": buf("u", BATCH * P),
            "wa": pair("wa", A_COLS), "wb": pair("wb", B_COLS), "wc": pair("wc", D),
            "cst": buf("cst", CST_COLS), "beta": buf("beta", P), "hw": buf("hw", 1),
            "ones": buf("ones", 2), "tiny": buf("tiny", 178), "powers": buf("powers", 2 * NCH),
        }
        ps = ctx.enter_context(nc.psum_tensor("ps", [P, 4096], F32))
        fills_set = ctx.enter_context(nc.semaphore("fills_set"))
        nc.gpsimd.memset(sb["ones"][:, :], 1.0).then_inc(fills_set, 1)
        nc.gpsimd.memset(sb["powers"][:, 0:NCH], -0.5).then_inc(fills_set, 1)
        nc.gpsimd.memset(sb["powers"][:, NCH:2 * NCH], 0.5).then_inc(fills_set, 1)
        nc.gpsimd.wait_ge(fills_set, 3)
        rows_loaded = {(rows, parity): ctx.enter_context(nc.semaphore(f"{rows}_rows_loaded{parity}"))
                       for rows in "abc" for parity in range(2)}
        setup_block(nc, io, sb, ps, ctx, rows_loaded)
        heads_block(nc, io, sb, ps, ctx, rows_loaded)


def shape_constants():
    h = np.ones((1, 1), np.float32)
    while h.shape[0] < P:
        h = np.block([[h, h], [h, -h]])
    cols = [h, np.eye(P, dtype=np.float32)]
    j = np.arange(P)[:, None]
    for l in range(LEVELS):
        i = np.array([n for n in range(P) if n >> l & 1])[None, :]
        cols.append(((j >> (l + 1) == i >> (l + 1)) & (j >> l & 1 == 0)).astype(np.float32))
    i = np.arange(P)[None, :]
    for m in range(SUB):
        cols.append(((j // SUB == i // SUB) & (j % SUB == m)).astype(np.float32))
    cols.append((j // SUB == np.arange(P // SUB)[None, :]).astype(np.float32))
    cols.append((j % SUB == np.arange(SUB)[None, :]).astype(np.float32))
    return np.ascontiguousarray(np.concatenate(cols, 1), np.float32)


def kernel(**inputs):
    import concourse.bacc as bacc
    from concourse.bass_utils import run_bass_kernel_spmd

    g = {n: np.asarray(v) for n, v in inputs.items()}
    at, ff = "L0_attn_", "L0_ffn_"

    def k_tiles(w):
        return w.reshape(KT, P, -1).transpose(1, 0, 2)

    def by_head(w):
        return w.reshape(KT, P, HEADS, P).transpose(2, 1, 0, 3).reshape(HEADS, P, KT * P)

    def rank(w):
        return w.reshape(P, HEADS, P).transpose(1, 0, 2)

    def per_channel(w):
        return w.reshape(HEADS, P, -1)

    def fill(n):
        return np.zeros((HEADS, P, n), np.float32)

    a_log = np.broadcast_to(g[at + "A_log"][:, None, None], (HEADS, P, 1))
    arrays = {
        "x": g[at + "hidden_states"].reshape(TOK, D),
        "consts": shape_constants(),
        "o_norm_w": g[at + "o_norm_w"].reshape(P, 1),
        "small_w": np.concatenate([k_tiles(g[at + n]).reshape(P, -1) for n in ("f_w1", "g_w1", "b_w")], 1),
        "ffn_consts": np.concatenate([
            g[ff + "SU_ug"].reshape(KT, P).T, g[ff + "SU_dp"].reshape(FT, P).T,
            g[ff + "Wscale_ug"].reshape(2 * FT, P).T, np.zeros((P, 6), np.float32),
            np.broadcast_to(g[ff + "Wscale_dp"][None, :], (P, D))], 1),
        "w_up": k_tiles(g[ff + "W_up"].T), "w_gate": k_tiles(g[ff + "W_gate"].T),
        "w_down": g[ff + "W_down"].T.reshape(FT, P, D).transpose(1, 0, 2).reshape(P, FT * D),
        "rows_a": np.concatenate([by_head(g[at + "q_w"]), by_head(g[at + "k_w"]), rank(g[at + "f_w2"]),
                                  per_channel(g[at + "q_conv_w"]), per_channel(g[at + "k_conv_w"]),
                                  per_channel(g[at + "dt_bias"]), a_log, fill(6)], 2).reshape(HEADS * P, A_COLS),
        "rows_b": np.concatenate([by_head(g[at + "v_w"]), rank(g[at + "g_w2"]), per_channel(g[at + "v_conv_w"]),
                                  per_channel(g[at + "g_b2"]), fill(11)], 2).reshape(HEADS * P, B_COLS),
        "o_w": g[at + "o_w"],
    }
    nc = bacc.Bacc("TRN2", target_bir_lowering=False, num_devices=1)
    feed, io = {}, {}
    for name, v in arrays.items():
        v = np.ascontiguousarray(v)
        feed["in_" + name] = v
        io[name] = nc.dram_tensor("in_" + name, v.shape, F32, kind="ExternalInput").ap()
    io["out"] = nc.dram_tensor("out", [TOK, D], F32, kind="ExternalOutput").ap()
    build(nc, io)
    r = run_bass_kernel_spmd(nc, [feed], core_ids=[0])
    return r.results[0]["out"].reshape(BATCH, SEQ, D)
```
